# Optimizing a Trainium2 kernel written in Bass

```python
import numpy as np
import jax
import jax.numpy as jnp

def _softmax(x, axis=-1):
    return jax.nn.softmax(x, axis=axis)

def _gelu(x):
    return jax.nn.gelu(x, approximate=True)

def _silu(x):
    return jax.nn.silu(x)

def _sigmoid(x):
    return jax.nn.sigmoid(x)

def _layernorm(x, axis=-1, eps=1e-05):
    m = jnp.mean(x, axis=axis, keepdims=True)
    v = jnp.var(x, axis=axis, keepdims=True)
    return (x - m) / jnp.sqrt(v + eps)

def _scatter_add(tgt, idx, src, axis=0):
    return tgt.at[idx].add(src)

def _segment_sum(src, seg, n):
    return jax.ops.segment_sum(src, seg, n)
kernel_name = 'mk_xattn_seq_d2_seqx_r8_09d013'

def setup_inputs(seed: int=0):
    np.random.seed(seed)
    _w = jnp.asarray

    def _rec_inputs():
        import jax
        import jax.numpy as jnp
        _rk = jax.random.key(seed)
        x = -0.0002928 + 1 * jax.random.normal(jax.random.fold_in(_rk, 1), (128, 64, 128), jnp.float32)
        _lenS = 64 - jax.random.randint(jax.random.fold_in(_rk, 7), (128,), 0, max(1, 64 // 4) + 1, jnp.int32)
        _lenS2 = 64 - jax.random.randint(jax.random.fold_in(_rk, 8), (128,), 0, max(1, 64 // 4) + 1, jnp.int32)
        _ctx_1024P = jax.random.normal(jax.random.fold_in(_rk, 11), (128, 16, 128), jnp.float32)
        _ctx_1024c = jax.random.dirichlet(jax.random.fold_in(_rk, 511), 0.3 * jnp.ones((16,), jnp.float32), (128, 64))
        _ctx_1024t = jnp.einsum('bsk,bkd->bsd', _ctx_1024c, _ctx_1024P)
        _ctx_1024t = _ctx_1024t * jax.lax.rsqrt(jnp.mean(jnp.square(_ctx_1024t)) + 1e-12) * 0.953939
        ctx_1024 = 4.13588e-05 + 0.999923 * (_ctx_1024t + 0.3 * jax.random.normal(jax.random.fold_in(_rk, 611), (128, 64, 128), jnp.float32))
        _validS = jnp.arange(64)[None, :] < _lenS[:, None]
        _validS2 = jnp.arange(64)[None, :] < _lenS2[:, None]
        _causal = jnp.tril(jnp.ones((64, 64), dtype=bool))
        mask_BxS2_bf1 = jnp.ones((128, 64), dtype=bool)
        mask_BxSxS_ik0 = jnp.where(jnp.broadcast_to(_validS[:, None, :], (128, 64, 64)), 0, 1).astype(jnp.int32)
        mask_BxSxS2_if1 = jnp.where(jnp.ones((128, 64, 64), dtype=bool), 1, 0).astype(jnp.int32)
        return (x, ctx_1024, mask_BxS2_bf1, mask_BxSxS_ik0, mask_BxSxS2_if1)
    x, ctx_1024, mask_BxS2_bf1, mask_BxSxS_ik0, mask_BxSxS2_if1 = _rec_inputs()

    def _L0_xattn_setup():
        import jax, jax.numpy as jnp
        import numpy as np
        NUM_HEADS = 16
        HEAD_DIM = 64
        D_MODEL = 128
        ROPE_BASE = 10000.0

        def rope(x):
            B, S, H, D = x.shape
            inv_freq = 1.0 / ROPE_BASE ** (jnp.arange(0, D, 2, dtype=jnp.float32) / D)
            t = jnp.arange(S, dtype=jnp.float32)
            freqs = jnp.einsum('s,d->sd', t, inv_freq)
            cos = jnp.cos(freqs)[None, :, None, :]
            sin = jnp.sin(freqs)[None, :, None, :]
            x1, x2 = (x[..., 0::2], x[..., 1::2])
            r1 = x1 * cos - x2 * sin
            r2 = x2 * cos + x1 * sin
            out = jnp.stack([r1, r2], axis=-1).reshape(B, S, H, D)
            return out.astype(x.dtype)
        key = jax.random.key(seed)
        ks = jax.random.split(key, 8)
        B, Sq, Skv = (4, 128, 256)
        d = D_MODEL
        hd = NUM_HEADS * HEAD_DIM
        scale = 1.0 / np.sqrt(d)
        return {'decoder_query': jax.random.normal(ks[0], (B, Sq, d), jnp.float32), 'encoder_key_value': jax.random.normal(ks[1], (B, Skv, d), jnp.float32), 'mask': jnp.ones((B, Skv), dtype=bool), 'Wq': jax.random.normal(ks[2], (d, hd), jnp.float32) * scale, 'Wk': jax.random.normal(ks[3], (d, hd), jnp.float32) * scale, 'Wv': jax.random.normal(ks[4], (d, hd), jnp.float32) * scale, 'Wo': jax.random.normal(ks[5], (hd, d), jnp.float32) * (1.0 / np.sqrt(hd)), 'ln_gamma': jnp.ones((d,), jnp.float32), 'ln_beta': jnp.zeros((d,), jnp.float32)}
    _L0_xattn_all = _L0_xattn_setup()
    _L0_xattn_in = {k: v for k, v in _L0_xattn_all.items() if k in ('Wq', 'Wk', 'Wv', 'Wo', 'ln_gamma', 'ln_beta')}
    del _L0_xattn_all

    def _L1_xattn_setup():
        import jax, jax.numpy as jnp
        import numpy as np
        B, T, S_ENC, D, H, E, K = (4, 128, 64, 128, 16, 8, 2)
        DK = D // H
        HID = 4 * D
        NEG = -65504.0
        EPS = 1e-05

        def rmsnorm(x, w):
            return w * (x * jax.lax.rsqrt(jnp.mean(x * x, axis=-1, keepdims=True) + EPS))

        def mha(xq, xk, xv, mask, wq, wk, wv, wo):
            q = jnp.einsum('bsd,ed->bse', xq, wq).reshape(xq.shape[0], -1, H, DK).transpose(0, 2, 1, 3)
            k = jnp.einsum('bsd,ed->bse', xk, wk).reshape(xk.shape[0], -1, H, DK).transpose(0, 2, 1, 3)
            v = jnp.einsum('bsd,ed->bse', xv, wv).reshape(xv.shape[0], -1, H, DK).transpose(0, 2, 1, 3)
            scores = jnp.einsum('bhqd,bhkd->bhqk', q, k) / jnp.sqrt(jnp.float32(DK))
            scores = jnp.where(mask[:, None, :, :] == 0, NEG, scores)
            attn = jax.nn.softmax(scores, axis=-1)
            out = jnp.einsum('bhqk,bhkd->bhqd', attn, v)
            out = out.transpose(0, 2, 1, 3).reshape(xq.shape[0], -1, D)
            return jnp.einsum('bsd,ed->bse', out, wo)

        def moe_ffn(x, gate_w, exp_w1, exp_w2, sh_w1, sh_w2):
            b, s, d = x.shape
            xf = x.reshape(-1, d)
            sh = jnp.einsum('nd,hd->nh', xf, sh_w1)
            sh = jax.nn.silu(sh)
            sh = jnp.einsum('nh,dh->nd', sh, sh_w2)
            logits = jnp.einsum('nd,ed->ne', xf, gate_w)
            topk_vals, topk_idx = jax.lax.top_k(logits, K)
            topk_gates = jax.nn.softmax(topk_vals, axis=-1)
            n = xf.shape[0]
            gates = jnp.zeros((n, E), dtype=xf.dtype).at[jnp.arange(n)[:, None], topk_idx].set(topk_gates)
            h = jnp.einsum('nd,ehd->neh', xf, exp_w1)
            h = jax.nn.silu(h)
            eo = jnp.einsum('neh,edh->ned', h, exp_w2)
            sel = jnp.einsum('ned,ne->nd', eo, gates)
            return (sh + sel).reshape(b, s, d)
        key = jax.random.key(seed)
        ks = jax.random.split(key, 16)
        sd = 1.0 / np.sqrt(D)
        inp = {'x': jax.random.normal(ks[0], (B, T, D), jnp.float32), 'encoder_output': jax.random.normal(ks[1], (B, S_ENC, D), jnp.float32), 'tgt_mask': jnp.tril(jnp.ones((T, T), jnp.int32))[None].repeat(B, 0), 'src_mask': jnp.ones((B, T, S_ENC), jnp.int32), 'norm1_w': jnp.ones((D,), jnp.float32), 'norm2_w': jnp.ones((D,), jnp.float32), 'norm3_w': jnp.ones((D,), jnp.float32), 'sa_wq': jax.random.normal(ks[2], (D, D), jnp.float32) * sd, 'sa_wk': jax.random.normal(ks[3], (D, D), jnp.float32) * sd, 'sa_wv': jax.random.normal(ks[4], (D, D), jnp.float32) * sd, 'sa_wo': jax.random.normal(ks[5], (D, D), jnp.float32) * sd, 'ca_wq': jax.random.normal(ks[6], (D, D), jnp.float32) * sd, 'ca_wk': jax.random.normal(ks[7], (D, D), jnp.float32) * sd, 'ca_wv': jax.random.normal(ks[8], (D, D), jnp.float32) * sd, 'ca_wo': jax.random.normal(ks[9], (D, D), jnp.float32) * sd, 'gate_w': jax.random.normal(ks[10], (E, D), jnp.float32) * 0.02, 'exp_w1': jax.random.normal(ks[11], (E, HID, D), jnp.float32) * sd, 'exp_w2': jax.random.normal(ks[12], (E, D, HID), jnp.float32) / np.sqrt(HID), 'sh_w1': jax.random.normal(ks[13], (HID, D), jnp.float32) * sd, 'sh_w2': jax.random.normal(ks[14], (D, HID), jnp.float32) / np.sqrt(HID)}
        return inp
    _L1_xattn_all = _L1_xattn_setup()
    _L1_xattn_in = {k: v for k, v in _L1_xattn_all.items() if k in ('norm1_w', 'norm2_w', 'norm3_w', 'sa_wq', 'sa_wk', 'sa_wv', 'sa_wo', 'ca_wq', 'ca_wk', 'ca_wv', 'ca_wo', 'gate_w', 'exp_w1', 'exp_w2', 'sh_w1', 'sh_w2')}
    del _L1_xattn_all
    return {'x': x, 'ctx_1024': ctx_1024, 'mask_BxS2_bf1': mask_BxS2_bf1, 'mask_BxSxS_ik0': mask_BxSxS_ik0, 'mask_BxSxS2_if1': mask_BxSxS2_if1, 'L0_xattn_Wq': _L0_xattn_in['Wq'], 'L0_xattn_Wk': _L0_xattn_in['Wk'], 'L0_xattn_Wv': _L0_xattn_in['Wv'], 'L0_xattn_Wo': _L0_xattn_in['Wo'], 'L0_xattn_ln_gamma': _L0_xattn_in['ln_gamma'], 'L0_xattn_ln_beta': _L0_xattn_in['ln_beta'], 'L1_xattn_norm1_w': _L1_xattn_in['norm1_w'], 'L1_xattn_norm2_w': _L1_xattn_in['norm2_w'], 'L1_xattn_norm3_w': _L1_xattn_in['norm3_w'], 'L1_xattn_sa_wq': _L1_xattn_in['sa_wq'], 'L1_xattn_sa_wk': _L1_xattn_in['sa_wk'], 'L1_xattn_sa_wv': _L1_xattn_in['sa_wv'], 'L1_xattn_sa_wo': _L1_xattn_in['sa_wo'], 'L1_xattn_ca_wq': _L1_xattn_in['ca_wq'], 'L1_xattn_ca_wk': _L1_xattn_in['ca_wk'], 'L1_xattn_ca_wv': _L1_xattn_in['ca_wv'], 'L1_xattn_ca_wo': _L1_xattn_in['ca_wo'], 'L1_xattn_gate_w': _L1_xattn_in['gate_w'], 'L1_xattn_exp_w1': _L1_xattn_in['exp_w1'], 'L1_xattn_exp_w2': _L1_xattn_in['exp_w2'], 'L1_xattn_sh_w1': _L1_xattn_in['sh_w1'], 'L1_xattn_sh_w2': _L1_xattn_in['sh_w2']}

def reference(x, ctx_1024, mask_BxS2_bf1, mask_BxSxS_ik0, mask_BxSxS2_if1, L0_xattn_Wq, L0_xattn_Wk, L0_xattn_Wv, L0_xattn_Wo, L0_xattn_ln_gamma, L0_xattn_ln_beta, L1_xattn_norm1_w, L1_xattn_norm2_w, L1_xattn_norm3_w, L1_xattn_sa_wq, L1_xattn_sa_wk, L1_xattn_sa_wv, L1_xattn_sa_wo, L1_xattn_ca_wq, L1_xattn_ca_wk, L1_xattn_ca_wv, L1_xattn_ca_wo, L1_xattn_gate_w, L1_xattn_exp_w1, L1_xattn_exp_w2, L1_xattn_sh_w1, L1_xattn_sh_w2):
    import jax
    import jax.numpy as jnp

    def _L0_xattn_ref(decoder_query, encoder_key_value, mask, Wq, Wk, Wv, Wo, ln_gamma, ln_beta):
        import jax, jax.numpy as jnp
        import numpy as np
        NUM_HEADS = 16
        HEAD_DIM = 64
        D_MODEL = 128
        ROPE_BASE = 10000.0

        def rope(x):
            B, S, H, D = x.shape
            inv_freq = 1.0 / ROPE_BASE ** (jnp.arange(0, D, 2, dtype=jnp.float32) / D)
            t = jnp.arange(S, dtype=jnp.float32)
            freqs = jnp.einsum('s,d->sd', t, inv_freq)
            cos = jnp.cos(freqs)[None, :, None, :]
            sin = jnp.sin(freqs)[None, :, None, :]
            x1, x2 = (x[..., 0::2], x[..., 1::2])
            r1 = x1 * cos - x2 * sin
            r2 = x2 * cos + x1 * sin
            out = jnp.stack([r1, r2], axis=-1).reshape(B, S, H, D)
            return out.astype(x.dtype)
        B, Sq, d = decoder_query.shape
        Skv = encoder_key_value.shape[1]
        H, Dh = (NUM_HEADS, HEAD_DIM)
        q = (decoder_query @ Wq).reshape(B, Sq, H, Dh)
        k = (encoder_key_value @ Wk).reshape(B, Skv, H, Dh)
        v = (encoder_key_value @ Wv).reshape(B, Skv, H, Dh)
        q = rope(q)
        k = rope(k)
        q = q.transpose(0, 2, 1, 3) * (1.0 / jnp.sqrt(jnp.asarray(Dh, q.dtype)))
        k = k.transpose(0, 2, 1, 3)
        v = v.transpose(0, 2, 1, 3)
        scores = jnp.einsum('bhqd,bhkd->bhqk', q, k)
        m = mask[:, None, None, :]
        scores = jnp.where(m, scores, jnp.asarray(-1000000000.0, scores.dtype))
        attn = jax.nn.softmax(scores, axis=-1)
        out = jnp.einsum('bhqk,bhkd->bqhd', attn, v).reshape(B, Sq, H * Dh)
        out = out @ Wo
        x = decoder_query + out
        mu = jnp.mean(x, axis=-1, keepdims=True)
        var = jnp.var(x, axis=-1, keepdims=True)
        y = (x - mu) * jax.lax.rsqrt(var + 0.001) * ln_gamma + ln_beta
        return y

    def _L1_xattn_ref(x, encoder_output, tgt_mask, src_mask, norm1_w, norm2_w, norm3_w, sa_wq, sa_wk, sa_wv, sa_wo, ca_wq, ca_wk, ca_wv, ca_wo, gate_w, exp_w1, exp_w2, sh_w1, sh_w2):
        import jax, jax.numpy as jnp
        import numpy as np
        B, T, S_ENC, D, H, E, K = (4, 128, 64, 128, 16, 8, 2)
        DK = D // H
        HID = 4 * D
        NEG = -65504.0
        EPS = 1e-05

        def rmsnorm(x, w):
            return w * (x * jax.lax.rsqrt(jnp.mean(x * x, axis=-1, keepdims=True) + EPS))

        def mha(xq, xk, xv, mask, wq, wk, wv, wo):
            q = jnp.einsum('bsd,ed->bse', xq, wq).reshape(xq.shape[0], -1, H, DK).transpose(0, 2, 1, 3)
            k = jnp.einsum('bsd,ed->bse', xk, wk).reshape(xk.shape[0], -1, H, DK).transpose(0, 2, 1, 3)
            v = jnp.einsum('bsd,ed->bse', xv, wv).reshape(xv.shape[0], -1, H, DK).transpose(0, 2, 1, 3)
            scores = jnp.einsum('bhqd,bhkd->bhqk', q, k) / jnp.sqrt(jnp.float32(DK))
            scores = jnp.where(mask[:, None, :, :] == 0, NEG, scores)
            attn = jax.nn.softmax(scores, axis=-1)
            out = jnp.einsum('bhqk,bhkd->bhqd', attn, v)
            out = out.transpose(0, 2, 1, 3).reshape(xq.shape[0], -1, D)
            return jnp.einsum('bsd,ed->bse', out, wo)

        def moe_ffn(x, gate_w, exp_w1, exp_w2, sh_w1, sh_w2):
            b, s, d = x.shape
            xf = x.reshape(-1, d)
            sh = jnp.einsum('nd,hd->nh', xf, sh_w1)
            sh = jax.nn.silu(sh)
            sh = jnp.einsum('nh,dh->nd', sh, sh_w2)
            logits = jnp.einsum('nd,ed->ne', xf, gate_w)
            topk_vals, topk_idx = jax.lax.top_k(logits, K)
            topk_gates = jax.nn.softmax(topk_vals, axis=-1)
            n = xf.shape[0]
            gates = jnp.zeros((n, E), dtype=xf.dtype).at[jnp.arange(n)[:, None], topk_idx].set(topk_gates)
            h = jnp.einsum('nd,ehd->neh', xf, exp_w1)
            h = jax.nn.silu(h)
            eo = jnp.einsum('neh,edh->ned', h, exp_w2)
            sel = jnp.einsum('ned,ne->nd', eo, gates)
            return (sh + sel).reshape(b, s, d)
        xn = rmsnorm(x, norm1_w)
        h = x + mha(xn, xn, xn, tgt_mask, sa_wq, sa_wk, sa_wv, sa_wo)
        hn = rmsnorm(h, norm2_w)
        h = h + mha(hn, encoder_output, encoder_output, src_mask, ca_wq, ca_wk, ca_wv, ca_wo)
        hn = rmsnorm(h, norm3_w)
        return h + moe_ffn(hn, gate_w, exp_w1, exp_w2, sh_w1, sh_w2)
    x = _L0_xattn_ref(x, ctx_1024, mask_BxS2_bf1, L0_xattn_Wq, L0_xattn_Wk, L0_xattn_Wv, L0_xattn_Wo, L0_xattn_ln_gamma, L0_xattn_ln_beta)
    x = _L1_xattn_ref(x, ctx_1024, mask_BxSxS_ik0, mask_BxSxS2_if1, L1_xattn_norm1_w, L1_xattn_norm2_w, L1_xattn_norm3_w, L1_xattn_sa_wq, L1_xattn_sa_wk, L1_xattn_sa_wv, L1_xattn_sa_wo, L1_xattn_ca_wq, L1_xattn_ca_wk, L1_xattn_ca_wv, L1_xattn_ca_wo, L1_xattn_gate_w, L1_xattn_exp_w1, L1_xattn_exp_w2, L1_xattn_sh_w1, L1_xattn_sh_w2)
    return x

_drawn_inputs = setup_inputs


def setup_inputs(seed=0):
    import zlib

    import numpy as np

    out = dict(_drawn_inputs(seed))
    spreads = {'L0_xattn_ln_gamma': (1.0, 0.2),
     'L0_xattn_ln_beta': (0.0, 0.1),
     'L1_xattn_norm1_w': (1.0, 0.2),
     'L1_xattn_norm2_w': (1.0, 0.2),
     'L1_xattn_norm3_w': (1.0, 0.2)}
    factors = {}
    for name, (base, spread) in spreads.items():
        noise = np.random.default_rng([zlib.crc32(name.encode()), seed]).standard_normal(out[name].shape)
        drawn = base * np.exp(spread * noise) if base else spread * noise
        out[name] = jnp.asarray(drawn.astype(out[name].dtype))
    for name, factor in factors.items():
        out[name] = (out[name] * factor).astype(out[name].dtype)
    return out
```

```python
import numpy as np
import concourse.bass as bass
from concourse import mybir
from contextlib import ExitStack

F32 = mybir.dt.float32
BF16 = mybir.dt.bfloat16
I32 = mybir.dt.int32
U8 = mybir.dt.uint8
ALU = mybir.AluOpType
ACT = mybir.ActivationFunctionType
AX = mybir.AxisListType

P = 128
S = 64
TILES = 4
G = TILES * P
B = G // S
H = 16
D0 = 64
D1 = 8
NC0 = H * D0 // P
E = 8
NE = E + 1
HC = 4
MASKED = -float(2.0 ** 100)
BIG = 3.0e38


def schedule():
    text = """
    V0 S0.0 V1 B0 S0.1 LG UP0 PT0.0 DN0 PV0.0 S0.2 UP1 PT0.1 W0.0 V2 DN1 PV0.1 LN0 S0.3 PT0.2 W0.1 RN1.0
    V3 UP2 PV0.2 LN1 XN1.0 LD PT0.3 DN2 W0.2 RN1.1 PV0.3 LN2 UP3 XN1.1 RN1.2 W0.3 DN3 XN1.2 LN3 QK0 QK1
    RN1.3 QK2 XN1.3 QK3 QV1 UP4 S1.0 DN4 QK4 S1.1 PT1.0 UP5 PV1.0 QK5 S1.2 PT1.1 ON1.0 DN5 PV1.1 QK6 W1.0
    S1.3 PT1.2 ON1.1 RN2.0 UP6 PV1.2 QK7 W1.1 XN2.0 PT1.3 ON1.2 RN2.1 DN6 PV1.3 W1.2 XN2.1 QK8 ON1.3 RN2.2
    QK9 W1.3 XN2.2 QK10 RN2.3 QK11 XN2.3 QK12 QV2 UP7 S2.0 DN7 QK13 S2.1 PT2.0 UP8 PV2.0 QK14 S2.2 PT2.1
    ON2.0 PV2.1 QK15 W2.0 S2.3 PT2.2 ON2.1 MB PV2.2 W2.1 PT2.3 ON2.2 DN8 PV2.3 W2.2 ON2.3 ST W2.3
    """
    steps = []
    for word in text.split():
        kind = word[:2] if word[:2] in ("MB", "LD", "QK", "B0", "LG", "UP", "DN", "PT", "PV", "LN", "RN", "XN",
                                        "QV", "ON", "ST") else word[0]
        rest = "" if kind == "B0" else word[len(kind):]
        steps.append((kind,) + tuple(int(v) for v in rest.split(".") if v))
    return steps


SCHEDULE = schedule()


def stage(step):
    return {"B0": "B", "LG": "B", "UP": "B", "DN": "B", "ST": "B", "MB": "C", "LD": "C", "QK": "C"}.get(step[0], "A")


def part(stages):
    return [s for s in SCHEDULE if stage(s) in stages]


def bank_uses():
    uses, n = {}, 0
    for s in SCHEDULE:
        count = {"LD": 2, "QK": 1, "V": 2, "QV": 3, "B0": 1, "LG": 1, "UP": HC}.get(s[0], 0)
        for part_of in range(count):
            uses[(s, part_of)] = f"proj{n % 2}"
            n += 1
        if s[0] in ("W", "XN", "ON"):
            uses[(s, 0)] = "work"
        if s[0] in ("PT", "PV"):
            for half in range(2 if s[0] == "PT" or s[1] == 0 else 1):
                uses[(s, half)] = f"turn{half}"
    assert n % 2 == 0
    return uses


BANK_OF = bank_uses()


def build(nc, x, ctx, m0, m1, m2, wq, wk, wv, wo, gamma, beta, norms, l1w, gw, w1, w2, cos, sin, ident,
          headmask, countdown, out):
    groups = x.shape[0] // G
    xg = x.rearrange("(g t p) d -> g p t d", t=TILES, p=P)
    cg = ctx.rearrange("(g t p) d -> g p t d", t=TILES, p=P)
    og = out.rearrange("(g t p) d -> g p t d", t=TILES, p=P)
    m0g = m0.rearrange("(g t b) k -> g b t k", t=TILES, b=2)
    m1g = m1.rearrange("(g t p) k -> g p t k", t=TILES, p=P)
    m2g = m2.rearrange("(g t p) k -> g p t k", t=TILES, p=P)

    with ExitStack() as stack:
        def sb(name, shape, dt=F32):
            return stack.enter_context(nc.sbuf_tensor(name, shape, dt))

        def sem(name):
            return stack.enter_context(nc.semaphore(name))

        wq_s, wk_s = sb("wq_s", [P, NC0, P]), sb("wk_s", [P, NC0, P])
        wv_s, wo_s = sb("wv_s", [P, H * D0]), sb("wo_s", [P, NC0, P])
        l1w_s = sb("l1w_s", [P, 8, P])
        gw_s = sb("gw_s", [P, E])
        w1_s, w2_s = sb("w1_s", [P, NE * HC, P]), sb("w2_s", [P, NE * HC, P])
        gamma_s, beta_s = sb("gamma_s", [P, P]), sb("beta_s", [P, P])
        norms_s = sb("norms_s", [P, 3])
        cos_s, sin_s = sb("cos_s", [P, S]), sb("sin_s", [P, S])
        ident_s, ident_b = sb("ident_s", [P, P]), sb("ident_b", [P, P], BF16)
        headmask_s = sb("headmask_s", [P, H // 2])
        countdown_s = sb("countdown_s", [P, E])
        halves = sb("halves", [P, 1])
        x_s, c_s = sb("x_s", [P, TILES, P]), sb("c_s", [P, TILES, P])
        residual = sb("residual", [P, TILES, P])
        m0_s = sb("m0_s", [P, TILES, S], U8)
        m1_s, m2_s = sb("m1_s", [P, TILES, S], I32), sb("m2_s", [P, TILES, S], I32)
        bias = sb("bias", [P, 3, TILES, S], BF16)
        xT, cT, cT1 = sb("xT", [P, G]), sb("cT", [P, G]), sb("cT1", [P, G])
        qk = sb("qk", [P, 2 * NC0, G])
        part_s, part_m = sb("part_s", [P, 2, 2, G]), sb("part_m", [P, 2, 2, G])
        v0 = sb("v0", [P, 2, 2, NC0, 2, D0])
        prob = sb("prob", [P, 2, H * S])
        probT = sb("probT", [P, NC0, P])
        attT = sb("attT", [P, NC0, P])
        rowmax, rowsum, rowinv = sb("rowmax", [P, H]), sb("rowsum", [P, H]), sb("rowinv", [P, H])
        nT = sb("nT", [P, G])
        q1 = sb("q1", [P, G])
        k1 = sb("k1", [P, B, H // 2, S])
        v1 = sb("v1", [P, TILES, 2, NC0, 2, D1 + 1])
        inv1 = sb("inv1", [P, H])
        o1, o1T = sb("o1", [P, P]), sb("o1T", [P, P])
        h = sb("h", [P, TILES, P])
        xn = sb("xn", [P, 2, P])
        square, total = sb("square", [P, P]), sb("total", [P, 1])
        var0, rstd0 = sb("var0", [P, TILES]), sb("rstd0", [P, TILES])
        var1, rstd1 = sb("var1", [P, 3, TILES]), sb("rstd1", [P, 3, TILES])
        mean0 = sb("mean0", [P, 1])
        hn3, hn3T = sb("hn3", [P, TILES, P]), sb("hn3T", [P, G])
        hid, tanh = sb("hid", [P, HC, G]), sb("tanh", [P, 2, G])
        acc = sb("acc", [P, TILES, P])
        weighted = sb("weighted", [P, 2, TILES, P])
        lg = sb("lg", [P, TILES, E])
        eq, key = sb("eq", [P, TILES, E]), sb("key", [P, TILES, E])
        first, second, lg2, gates = (sb(n, [P, TILES, E]) for n in ("first", "second", "lg2", "gates"))
        top1, top2, keymax, gap, e2, den, g1, g2 = (
            sb(n, [P, TILES]) for n in ("top1", "top2", "keymax", "gap", "e2", "den", "g1", "g2"))

        proj = stack.enter_context(nc.psum_tensor("proj", [P, 2, 512], F32))
        score = stack.enter_context(nc.psum_tensor("score", [P, 2, 512], F32))
        turn = stack.enter_context(nc.psum_tensor("turn", [P, 2, 512], F32))
        down = stack.enter_context(nc.psum_tensor("down", [P, 512], F32))
        work = stack.enter_context(nc.psum_tensor("work", [P, 512], F32))

        def pj(step, n):
            return proj[:, int(BANK_OF[(step, n)][-1]), :]

        per = {}

        def counted(name, n):
            s = sem(name)
            per[name] = (s, n)
            return name

        for name, n in (
            ("pe_xc", 2), ("pe_qk", 2 * NC0), ("pe_v", TILES), ("pe_s", 3 * TILES), ("pe_pt", 6 * TILES),
            ("pe_pv0", 2 * TILES), ("pe_pv1", 2 * TILES), ("pe_on", 2 * TILES), ("pe_w", 3 * TILES),
            ("pe_xn", 2 * TILES), ("pe_qv", 6), ("pe_h3", 1), ("pe_lg", 1), ("pe_up", NE * HC), ("pe_dn", NE),
            ("act_xc", 2), ("act_v", TILES), ("act_exp", 3 * TILES), ("act_pt", 6 * TILES), ("act_ot", 2 * TILES),
            ("act_on", 2 * TILES), ("act_xn", 2 * TILES), ("act_q1", 2), ("act_v1", 2), ("act_h3", 1),
            ("act_e2", 1), ("act_tanh", NE * HC), ("act_cT1", 1), ("act_k1", 2),
            ("dve_bias", 3), ("dve_cos", 2 * NC0), ("dve_sin", 2 * NC0), ("dve_sub", 3 * TILES),
            ("dve_inv", TILES), ("dve_k1", 2), ("dve_on", 2 * TILES), ("dve_w", 3 * TILES),
            ("dve_var0", TILES), ("dve_var1", 3 * TILES), ("dve_ln", TILES), ("dve_xn", 2 * TILES), ("dve_hn3", 1),
            ("dve_lg", 1), ("dve_hid", NE * HC), ("dve_gap", 1), ("dve_gates", 1), ("dve_wt", NE),
            ("pool_qk", 2 * NC0), ("pool_norm", TILES), ("pool_rstd0", TILES), ("pool_rstd1", 3 * TILES),
            ("pool_acc", NE),
        ):
            counted(name, n)
        s_w0, s_wv, s_w1, s_w2, s_l1 = sem("load_wqk"), sem("load_wv"), sem("load_w1"), sem("load_w2"), sem("load_l1")
        s_tab = sem("load_tables")
        s_x, s_c, s_m, s_res = sem("load_x"), sem("load_ctx"), sem("load_masks"), sem("load_residual")
        s_move = [sem("partners_moved0"), sem("partners_moved1")]
        s_out = sem("stored")
        s_init, s_idb = sem("buffers_initialised"), sem("identity_bf16")
        s_chainA, s_chainB = sem("vector_chain_a"), sem("vector_chain_b")

        def after(eng, name, it, n):
            s, k = per[name]
            eng.wait_ge(s, it * k + (n + 1))

        def done(ins, name):
            ins.then_inc(per[name][0], 1)

        def is_zero(it):
            return isinstance(it, int) and it == 0

        def readers(step, n):
            kind = step[0]
            if kind == "LD":
                return [("act_xc", n)]
            if kind == "QK":
                return [("dve_sin", step[1])]
            if kind == "V":
                return [("act_v", step[1])]
            if kind == "QV":
                g = step[1] - 1
                return ([("act_q1", g)], [("act_k1", g)], [("act_v1", g)])[n]
            if kind == "B0":
                return [("act_h3", 0)]
            if kind == "LG":
                return [("dve_lg", 0)]
            if kind == "UP":
                return [("dve_hid", HC * step[1] + n)]
            if kind == "W":
                return [("dve_w", TILES * step[1] + step[2])]
            if kind == "XN":
                return [("act_xn", TILES * (step[1] - 1) + step[2])]
            if kind == "ON":
                return [("act_on", TILES * (step[1] - 1) + step[2])]
            if kind == "PT":
                return [("act_pt", 2 * (TILES * step[1] + step[2]) + n)]
            if kind == "PV":
                return [("act_ot", 2 * step[2] + n) if step[1] == 0 else ("dve_on", TILES * (step[1] - 1) + step[2])]

        def bank_free(pe, steps, step, n, of):
            bank = BANK_OF[(step, n)]
            uses = [(s, m) for s in steps for m in range(HC) if BANK_OF.get((s, m)) == bank]
            at = uses.index((step, n))
            if at:
                s, m = uses[at - 1]
                for name, k in readers(s, m):
                    after(pe, name, of[stage(s)], k)
                return
            for st in "ABC":
                mine = [(s, m) for s in SCHEDULE for m in range(HC) if BANK_OF.get((s, m)) == bank and stage(s) == st]
                if mine and not is_zero(of[st]):
                    for name, _ in readers(*mine[-1]):
                        sm, count = per[name]
                        pe.wait_ge(sm, of[st] * count)

        block = stack.enter_context(nc.Block())

        @block.sync
        def _(sp):
            sp.dma_start(cos_s[:], cos).then_inc(s_tab, 16)
            sp.dma_start(sin_s[:], sin).then_inc(s_tab, 16)
            sp.dma_start(ident_s[:], ident).then_inc(s_tab, 16)
            sp.dma_start(headmask_s[:], headmask).then_inc(s_tab, 16)
            sp.dma_start(countdown_s[:], countdown).then_inc(s_tab, 16)
            sp.dma_start(gamma_s[:], gamma.partition_broadcast(P)).then_inc(s_tab, 16)
            sp.dma_start(beta_s[:], beta.partition_broadcast(P)).then_inc(s_tab, 16)
            sp.dma_start(norms_s[:], norms).then_inc(s_tab, 16)

            def iteration(ia, first):
                def released(name, n):
                    if not first:
                        after(sp, name, ia - 1, n)

                released("pe_xc", 1)
                sp.dma_start(x_s[:], xg[ia]).then_inc(s_x, 16)
                sp.dma_start(c_s[:], cg[ia]).then_inc(s_c, 16)
                released("dve_w", TILES - 1)
                sp.dma_start(residual[:], xg[ia]).then_inc(s_res, 16)
                for b in range(2):
                    sp.dma_start(m0_s[b * S:(b + 1) * S], m0g[ia, b].partition_broadcast(S)).then_inc(s_m, 16)
                sp.dma_start(m1_s[:], m1g[ia]).then_inc(s_m, 16)
                sp.dma_start(m2_s[:], m2g[ia]).then_inc(s_m, 16)
                if first:
                    sp.dma_start(wq_s[:], wq).then_inc(s_w0, 16)
                    sp.dma_start(wk_s[:], wk).then_inc(s_w0, 16)
                    sp.dma_start(wv_s[:], wv).then_inc(s_wv, 16)
                    sp.dma_start(wo_s[:], wo).then_inc(s_wv, 16)
                    sp.dma_start(l1w_s[:], l1w).then_inc(s_l1, 16)
                    sp.dma_start(gw_s[:], gw).then_inc(s_l1, 16)
                    sp.dma_start(w1_s[:], w1).then_inc(s_w1, 16)
                    sp.dma_start(w2_s[:], w2).then_inc(s_w2, 16)
                for pair in range(NC0):
                    after(sp, "dve_sin", ia, 2 * pair + 1)
                    r = pair % 2
                    for quad in range(4):
                        to = quad ^ 1
                        sp.dma_start(part_m[32 * to:32 * to + 32, r], part_s[32 * quad:32 * quad + 32, r])\
                          .then_inc(s_move[r], 16)

            iteration(0, True)
            iteration(1, False)
            with sp.Fori(2, groups) as i:
                iteration(i, False)

        @block.gpsimd
        def _(pool):
            nc.gpsimd.memset(halves[:], -0.5).then_inc(s_init, 1)
            nc.gpsimd.memset(v0[:], 0.0).then_inc(s_init, 1)
            nc.gpsimd.memset(v1[:], 0.0).then_inc(s_init, 1)
            pool.wait_ge(s_init, 3)
            for cc in range(2):
                nc.gpsimd.memset(v1[cc * S:(cc + 1) * S, :, :, :, cc, D1:D1 + 1], 1.0).then_inc(s_init, 1)
            pool.wait_ge(s_init, 5)

            def iteration(ia, ib, ic, steps):
                for step in steps:
                    kind = step[0]
                    if kind == "QK" and step[1] % 2:
                        pair = step[1] // 2
                        pool.wait_ge(s_move[pair % 2], 64 * (pair // 2 + 1) + ic * (64 * NC0 // 2))
                        for c in range(2):
                            n = 2 * pair + c
                            done(nc.gpsimd.tensor_tensor(qk[:, n], qk[:, n], part_m[:, pair % 2, c], ALU.add), "pool_qk")
                    elif kind == "PT" and step[1] == 0:
                        t = step[2]
                        after(pool, "dve_inv", ia, t)
                        pr = prob[:, t % 2].rearrange("p (h k) -> p h k", h=H)
                        done(nc.gpsimd.tensor_tensor(pr, pr, rowinv[:].unsqueeze(2).to_broadcast([P, H, S]), ALU.mult),
                             "pool_norm")
                    elif kind == "W":
                        a, t = step[1:]
                        if a == 0:
                            after(pool, "dve_var0", ia, t)
                            done(nc.gpsimd.tensor_tensor(rstd0[:, t:t + 1], var0[:, t:t + 1], halves[:], ALU.pow), "pool_rstd0")
                        else:
                            after(pool, "dve_var1", ia, TILES * a + t)
                            done(nc.gpsimd.tensor_tensor(rstd1[:, a, t:t + 1], var1[:, a, t:t + 1], halves[:], ALU.pow),
                                 "pool_rstd1")
                    elif kind == "LN":
                        t = step[1]
                        after(pool, "dve_var1", ia, t)
                        done(nc.gpsimd.tensor_tensor(rstd1[:, 0, t:t + 1], var1[:, 0, t:t + 1], halves[:], ALU.pow),
                             "pool_rstd1")
                    elif kind == "B0":
                        pass
                    elif kind == "DN":
                        e = step[1]
                        after(pool, "dve_wt", ib, e)
                        if e == 0:
                            if not is_zero(ib):
                                pool.wait_ge(s_out, ib * 16)
                        else:
                            after(pool, "pool_acc", ib, e - 1)
                        done(nc.gpsimd.tensor_tensor(acc[:], acc[:] if e else h[:], weighted[:, e % 2], ALU.add), "pool_acc")

            iteration(0, 0, 0, part("C"))
            iteration(0, 0, 1, part("AC"))
            iteration(1, 0, 2, part("ABC"))
            with pool.Fori(2, groups - 1) as i:
                iteration(i, i - 1, i + 1, part("ABC"))
            iteration(groups - 1, groups - 2, groups, part("AB"))
            iteration(groups, groups - 1, groups, part("B"))

        @block.scalar
        def _(act):
            def iteration(ia, ib, ic, steps):
                for step in steps:
                    kind = step[0]
                    if kind == "LD":
                        if not is_zero(ic):
                            after(act, "pe_v", ic - 1, TILES - 1)
                        for n, dst in enumerate((xT, cT)):
                            after(act, "pe_xc", ic, n)
                            done(nc.scalar.copy(dst[:], pj(step, n)), "act_xc")
                    elif kind == "V":
                        t = step[1]
                        after(act, "pe_v", ia, t)
                        if is_zero(ia) and t == 0:
                            act.wait_ge(s_init, 5)
                        if t >= 2:
                            after(act, "pe_pv0", ia, 2 * (t - 2) + 1)
                        elif not is_zero(ia):
                            after(act, "pe_pv0", ia - 1, 2 * (t + 2) + 1)
                        n0, n1 = (int(BANK_OF[(step, n)][-1]) for n in range(2))
                        assert (n0, n1) == (0, 1)
                        for b in range(2):
                            for cc in range(2):
                                src = proj[b * S:(b + 1) * S].rearrange("p n (j c d) -> p (n j) c d", c=2, d=D0)[:, :, cc]
                                ins = nc.scalar.copy(v0[cc * S:(cc + 1) * S, t % 2, b, :, cc], src)
                        done(ins, "act_v")
                        if t == 0:
                            if not is_zero(ia):
                                after(act, "pe_qv", ia - 1, 5)
                            after(act, "act_xc", ia, 1)
                            done(nc.scalar.copy(cT1[:], cT[:]), "act_cT1")
                    elif kind == "S":
                        a, t = step[1:]
                        after(act, "dve_sub", ia, TILES * a + t)
                        done(nc.scalar.activation(prob[:, t % 2], prob[:, t % 2], ACT.Exp,
                                                  scale=float((D1 if a else D0) ** -0.5)), "act_exp")
                    elif kind == "PT":
                        a, t = step[1:]
                        for half in range(2):
                            after(act, "pe_pt", ia, 2 * (TILES * a + t) + half)
                            done(nc.scalar.copy(probT[:, 4 * half:4 * half + 4], turn[:, half, :]), "act_pt")
                    elif kind == "PV" and step[1] == 0:
                        t = step[2]
                        for half in range(2):
                            after(act, "pe_pv0", ia, 2 * t + half)
                            if t:
                                after(act, "pe_w", ia, t - 1)
                            elif not is_zero(ia):
                                after(act, "pe_w", ia - 1, TILES - 1)
                            done(nc.scalar.copy(attT[:, 4 * half:4 * half + 4], turn[:, half, :]), "act_ot")
                    elif kind == "XN":
                        a, t = step[1:]
                        after(act, "pe_xn", ia, TILES * (a - 1) + t)
                        if is_zero(ia) and a == 1 and t == 0:
                            act.wait_ge(s_tab, 8 * 16)
                        done(nc.scalar.mul(nT[:, t * P:(t + 1) * P], work[:, 0:P], norms_s[:, a - 1:a]), "act_xn")
                    elif kind == "QV":
                        a = step[1]
                        after(act, "pe_qv", ia, 3 * (a - 1))
                        done(nc.scalar.copy(q1[:], pj(step, 0)), "act_q1")
                        after(act, "pe_qv", ia, 3 * (a - 1) + 1)
                        done(nc.scalar.copy(k1[:, :, H // 2 - 1], pj(step, 1).rearrange("p (b s) -> p b s", b=B)), "act_k1")
                        after(act, "pe_qv", ia, 3 * (a - 1) + 2)
                        src = pj(step, 2).rearrange("p (t j c d) -> p t j c d", t=TILES, c=2, d=D1)
                        for b in range(2):
                            for cc in range(2):
                                ins = nc.scalar.copy(v1[cc * S:(cc + 1) * S, :, b, :, cc, 0:D1],
                                                     src[b * S:(b + 1) * S, :, :, cc])
                        done(ins, "act_v1")
                    elif kind == "ON":
                        a, t = step[1:]
                        after(act, "pe_on", ia, TILES * (a - 1) + t)
                        done(nc.scalar.copy(o1T[:], work[:, 0:P]), "act_on")
                    elif kind == "B0":
                        after(act, "pe_h3", ib, 0)
                        done(nc.scalar.mul(hn3T[:], pj(step, 0), norms_s[:, 2:3]), "act_h3")
                    elif kind == "LG":
                        after(act, "dve_gap", ib, 0)
                        done(nc.scalar.activation(e2[:], gap[:], ACT.Exp), "act_e2")
                    elif kind == "UP":
                        e = step[1]
                        for c in range(HC):
                            after(act, "pe_up", ib, HC * e + c)
                            if HC * e + c >= 2:
                                after(act, "dve_hid", ib, HC * e + c - 2)
                            elif not is_zero(ib):
                                after(act, "dve_hid", ib - 1, HC * NE + c - 2)
                            done(nc.scalar.activation(tanh[:, c % 2], pj(step, c), ACT.Tanh, scale=0.5), "act_tanh")
                    elif kind == "ST":
                        after(act, "pool_acc", ib, NE - 1)
                        act.dma_start(og[ib], acc[:]).then_inc(s_out, 16)

            iteration(0, 0, 0, part("C"))
            iteration(0, 0, 1, part("AC"))
            iteration(1, 0, 2, part("ABC"))
            with act.Fori(2, groups - 1) as i:
                iteration(i, i - 1, i + 1, part("ABC"))
            iteration(groups - 1, groups - 2, groups, part("AB"))
            iteration(groups, groups - 1, groups, part("B"))
            act.wait_ge(s_out, groups * 16)

        LINKS_A, LINKS_B = 58, 18

        @block.vector
        def _(dve):
            dve.wait_ge(s_tab, 8 * 16)
            nc.vector.tensor_copy(ident_b[:], ident_s[:]).then_inc(s_idb, 1)

            def iteration(ia, ib, ic, steps):
                links = {"A": 0, "B": 0}

                def link(ins, which="A"):
                    s, it, k = (s_chainA, ia, LINKS_A) if which == "A" else (s_chainB, ib, LINKS_B)
                    links[which] += 1
                    ins.then_inc(s, 1)
                    dve.wait_ge(s, it * k + links[which])

                def mean_square(src, dst, a, t):
                    link(nc.vector.tensor_tensor_reduce(out=square[:], in0=src, in1=src, scale=1.0, scalar=0.0,
                                                        op0=ALU.mult, op1=ALU.add, accum_out=total[:]))
                    done(nc.vector.tensor_scalar(dst, total[:], 1.0 / P, 1e-5, ALU.mult, ALU.add), "dve_var1")

                for step in steps:
                    kind = step[0]
                    if kind == "MB":
                        dve.wait_ge(s_m, 64 * (ic + 1))
                        if not is_zero(ic):
                            after(dve, "pe_s", ic - 1, 3 * TILES - 1)
                        for n, m in enumerate((m0_s, m1_s, m2_s)):
                            done(nc.vector.tensor_scalar(bias[:, n], m[:], 0.0, MASKED, ALU.is_equal, ALU.mult), "dve_bias")
                    elif kind == "QK":
                        n = step[1]
                        after(dve, "pe_qk", ic, n)
                        pair = n // 2
                        if not is_zero(ic):
                            after(dve, "pe_s", ic - 1, TILES - 1)
                        src = pj(step, 0).rearrange("p (b s) -> p b s", b=B)
                        tab = [tb[:].unsqueeze(1).to_broadcast([P, B, S]) for tb in (cos_s, sin_s)]
                        done(nc.vector.tensor_tensor(qk[:, n].rearrange("p (b s) -> p b s", b=B), src, tab[0], ALU.mult),
                             "dve_cos")
                        if pair >= 2:
                            after(dve, "pool_qk", ic, 2 * (pair - 2) + 1)
                        elif not is_zero(ic):
                            after(dve, "pool_qk", ic - 1, 2 * (pair + NC0 - 2) + 1)
                        done(nc.vector.tensor_tensor(part_s[:, pair % 2, n % 2].rearrange("p (b s) -> p b s", b=B),
                                                     src, tab[1], ALU.mult), "dve_sin")
                    elif kind == "S":
                        a, t = step[1:]
                        after(dve, "pe_s", ia, TILES * a + t)
                        sc = score[:].rearrange("p n (h k) -> p (n h) k", k=S)
                        pr = prob[:, t % 2].rearrange("p (h k) -> p h k", h=H)
                        link(nc.vector.tensor_reduce(rowmax[:], sc, AX.X, ALU.max))
                        if a or t >= 2:
                            after(dve, "pe_pt", ia, 2 * (TILES * a + t - 2) + 1)
                        elif not is_zero(ia):
                            after(dve, "pe_pt", ia - 1, 2 * (3 * TILES + t - 2) + 1)
                        done(nc.vector.tensor_tensor(pr, sc, rowmax[:].unsqueeze(2).to_broadcast([P, H, S]), ALU.subtract),
                             "dve_sub")
                        if a == 0:
                            after(dve, "act_exp", ia, t)
                            link(nc.vector.tensor_reduce(rowsum[:], pr, AX.X, ALU.add))
                            if t:
                                after(dve, "pool_norm", ia, t - 1)
                            done(nc.vector.reciprocal(rowinv[:], rowsum[:]), "dve_inv")
                    elif kind == "W":
                        a, t = step[1:]
                        after(dve, "pe_w", ia, TILES * a + t)
                        ht = h[:, t]
                        if a == 0:
                            if t == 0:
                                dve.wait_ge(s_res, 16 * (ia + 1))
                            if t == 0 and not is_zero(ia):
                                after(dve, "pool_acc", ib, 0)
                            done(nc.vector.tensor_tensor(ht, residual[:, t], work[:, 0:P], ALU.add), "dve_w")
                            after(dve, "dve_w", ia, t)
                            link(nc.vector.tensor_reduce(total[:], ht, AX.X, ALU.add))
                            link(nc.vector.tensor_scalar(mean0[:], total[:], 1.0 / P, None, ALU.mult))
                            link(nc.vector.tensor_scalar(ht, ht, mean0[:], None, ALU.subtract))
                            link(nc.vector.tensor_tensor_reduce(out=square[:], in0=ht, in1=ht, scale=1.0, scalar=0.0,
                                                                op0=ALU.mult, op1=ALU.add, accum_out=total[:]))
                            done(nc.vector.tensor_scalar(var0[:, t:t + 1], total[:], 1.0 / P, 1e-3, ALU.mult, ALU.add),
                                 "dve_var0")
                        else:
                            done(nc.vector.tensor_tensor(ht, ht, work[:, 0:P], ALU.add), "dve_w")
                            after(dve, "dve_w", ia, TILES * a + t)
                            mean_square(ht, var1[:, a, t:t + 1], a, t)
                    elif kind == "LN":
                        t = step[1]
                        ht = h[:, t]
                        after(dve, "pool_rstd0", ia, t)
                        link(nc.vector.scalar_tensor_tensor(out=ht, in0=ht, scalar=rstd0[:, t:t + 1], in1=gamma_s[:],
                                                            op0=ALU.mult, op1=ALU.mult))
                        done(nc.vector.tensor_tensor(ht, ht, beta_s[:], ALU.add), "dve_ln")
                        after(dve, "dve_ln", ia, t)
                        mean_square(ht, var1[:, 0, t:t + 1], 0, t)
                    elif kind == "RN":
                        a, t = step[1:]
                        after(dve, "pool_rstd1", ia, TILES * (a - 1) + t)
                        if t >= 2:
                            after(dve, "pe_xn", ia, TILES * (a - 1) + t - 2)
                        done(nc.vector.tensor_scalar(xn[:, t % 2], h[:, t], rstd1[:, a - 1, t:t + 1], None, ALU.mult),
                             "dve_xn")
                    elif kind == "QV":
                        a = step[1]
                        after(dve, "act_k1", ia, a - 1)
                        kp = k1[:, :, H // 2 - 1]
                        for hh in range(H // 2):
                            if hh == H // 2 - 1:
                                link(ins)
                            ins = nc.vector.tensor_scalar(k1[:, :, hh], kp, headmask_s[:, hh:hh + 1], None, ALU.mult)
                        done(ins, "dve_k1")
                    elif kind == "PV" and step[1]:
                        a, t = step[1:]
                        after(dve, "pe_pv1", ia, TILES * (a - 1) + t)
                        o = turn[:, 0, 0:H * (D1 + 1)].rearrange("p (h d) -> p h d", h=H)
                        link(nc.vector.reciprocal(inv1[:], o[:, :, D1]))
                        if t or a > 1:
                            after(dve, "pe_on", ia, TILES * (a - 1) + t - 1)
                        done(nc.vector.tensor_tensor(o1[:].rearrange("p (h d) -> p h d", h=H), o[:, :, 0:D1],
                                                     inv1[:].unsqueeze(2).to_broadcast([P, H, D1]), ALU.mult), "dve_on")
                    elif kind == "B0":
                        after(dve, "pool_rstd1", ib, 3 * TILES - 1)
                        for t in range(TILES):
                            ins = nc.vector.tensor_scalar(hn3[:, t], h[:, t], rstd1[:, 2, t:t + 1], None, ALU.mult)
                        done(ins, "dve_hn3")
                    elif kind == "LG":
                        def wide(v):
                            return v[:].unsqueeze(2).to_broadcast([P, TILES, E])
                        cd = countdown_s[:].unsqueeze(1).to_broadcast([P, TILES, E])
                        after(dve, "pe_lg", ib, 0)
                        done(nc.vector.tensor_copy(lg[:], pj(step, 0)[:, 0:TILES * E].rearrange("p (t e) -> p t e", e=E)), "dve_lg")
                        after(dve, "dve_lg", ib, 0)
                        for src, top, pick in ((lg, top1, first_of["first"]), (lg2, top2, first_of["second"])):
                            link(nc.vector.tensor_reduce(top[:], src[:], AX.X, ALU.max), "B")
                            link(nc.vector.tensor_tensor(eq[:], src[:], wide(top), ALU.is_equal), "B")
                            link(nc.vector.tensor_tensor(key[:], eq[:], cd, ALU.mult), "B")
                            link(nc.vector.tensor_reduce(keymax[:], key[:], AX.X, ALU.max), "B")
                            link(nc.vector.tensor_tensor(pick[:], key[:], wide(keymax), ALU.is_equal), "B")
                            if src is lg:
                                link(nc.vector.tensor_scalar(lg2[:], pick[:], -BIG, None, ALU.mult), "B")
                                link(nc.vector.tensor_tensor(lg2[:], lg2[:], lg[:], ALU.add), "B")
                        done(nc.vector.tensor_tensor(gap[:], top2[:], top1[:], ALU.subtract), "dve_gap")
                        after(dve, "act_e2", ib, 0)
                        link(nc.vector.tensor_scalar_add(den[:], e2[:], 1.0), "B")
                        link(nc.vector.reciprocal(g1[:], den[:]), "B")
                        link(nc.vector.tensor_scalar(g1[:], g1[:], 0.5, None, ALU.mult), "B")
                        link(nc.vector.tensor_tensor(g2[:], e2[:], g1[:], ALU.mult), "B")
                        link(nc.vector.tensor_tensor(gates[:], first_of["first"][:], wide(g1), ALU.mult), "B")
                        link(nc.vector.tensor_tensor(key[:], first_of["second"][:], wide(g2), ALU.mult), "B")
                        done(nc.vector.tensor_tensor(gates[:], gates[:], key[:], ALU.add), "dve_gates")
                    elif kind == "UP":
                        e = step[1]
                        if e:
                            after(dve, "pe_dn", ib, e - 1)
                        elif not is_zero(ib):
                            after(dve, "pe_dn", ib - 1, NE - 1)
                        for c in range(HC):
                            after(dve, "act_tanh", ib, HC * e + c)
                            done(nc.vector.scalar_tensor_tensor(out=hid[:, c], in0=tanh[:, c % 2], scalar=1.0, in1=pj(step, c),
                                                                op0=ALU.add, op1=ALU.mult), "dve_hid")
                    elif kind == "DN":
                        e = step[1]
                        after(dve, "pe_dn", ib, e)
                        if e >= 2:
                            after(dve, "pool_acc", ib, e - 2)
                        src = down[:].rearrange("p (t d) -> p t d", t=TILES)
                        if e == 0:
                            done(nc.vector.tensor_scalar(weighted[:, 0], src, 0.5, None, ALU.mult), "dve_wt")
                        else:
                            if e == 1:
                                after(dve, "dve_gates", ib, 0)
                            done(nc.vector.tensor_tensor(weighted[:, e % 2], src,
                                                         gates[:, :, e - 1:e].to_broadcast([P, TILES, P]), ALU.mult), "dve_wt")
                assert links["A"] in (0, LINKS_A) and links["B"] in (0, LINKS_B), links

            first_of = {"first": first, "second": second}
            iteration(0, 0, 0, part("C"))
            iteration(0, 0, 1, part("AC"))
            iteration(1, 0, 2, part("ABC"))
            with dve.Fori(2, groups - 1) as i:
                iteration(i, i - 1, i + 1, part("ABC"))
            iteration(groups - 1, groups - 2, groups, part("AB"))
            iteration(groups, groups - 1, groups, part("B"))

        @block.tensor
        def _(pe):
            def iteration(ia, ib, ic, steps):
                for step in steps:
                    kind = step[0]

                    def free(n=0):
                        bank_free(pe, steps, step, n, {"A": ia, "B": ib, "C": ic})

                    if kind == "LD":
                        for n, (src, s) in enumerate(((x_s, s_x), (c_s, s_c))):
                            if is_zero(ic):
                                pe.wait_ge(s_tab, 8 * 16)
                            pe.wait_ge(s, 16 * (ic + 1))
                            free(n)
                            for t in range(TILES):
                                ins = nc.tensor.transpose(pj(step, n)[:, t * P:(t + 1) * P], src[:, t], ident_s[:])
                            done(ins, "pe_xc")
                    elif kind == "QK":
                        n = step[1]
                        free()
                        if n == 0:
                            after(pe, "act_xc", ic, 1)
                            if is_zero(ic):
                                pe.wait_ge(s_w0, 32)
                        w, src = (wq_s, xT) if n < NC0 else (wk_s, cT)
                        done(nc.tensor.matmul(pj(step, 0), w[:, n % NC0], src[:], start=True, stop=True), "pe_qk")
                    elif kind == "V":
                        t = step[1]
                        if is_zero(ia) and t == 0:
                            pe.wait_ge(s_wv, 32)
                        for n in range(2):
                            free(n)
                            ins = nc.tensor.matmul(pj(step, n), cT[:, t * P:(t + 1) * P], wv_s[:, n * 512:(n + 1) * 512],
                                                   start=True, stop=True)
                        done(ins, "pe_v")
                    elif kind == "S":
                        a, t = step[1:]
                        if a or t:
                            after(pe, "dve_sub", ia, TILES * a + t - 1)
                        elif not is_zero(ia):
                            after(pe, "dve_sub", ia - 1, 3 * TILES - 1)
                        if t == 0:
                            if a == 0:
                                after(pe, "dve_bias", ia, 2)
                                after(pe, "pool_qk", ia, 2 * NC0 - 1)
                                if is_zero(ia):
                                    pe.wait_ge(s_idb, 1)
                            else:
                                after(pe, "act_q1", ia, a - 1)
                                after(pe, "dve_k1", ia, a - 1)
                        for hp in range(2):
                            nc.tensor.matmul(score[:, hp].rearrange("p (h k) -> p h k", k=S), ident_b[:],
                                             bias[:, a, t].unsqueeze(1).to_broadcast([P, H // 2, S]), start=True, stop=True)
                        ts = t * P
                        if a == 0:
                            for c in range(NC0):
                                for hp in range(2):
                                    for b in range(2):
                                        rows = slice(hp * D0, hp * D0 + D0)
                                        tok = slice(ts + b * S, ts + b * S + S)
                                        ins = nc.tensor.matmul(score[b * S:(b + 1) * S, hp, c * S:(c + 1) * S],
                                                               qk[rows, c, tok], qk[rows, NC0 + c, tok],
                                                               start=False, stop=True, skip_group_check=True)
                        else:
                            for b in range(2):
                                for hp in range(2):
                                    rows = slice(hp * 64, hp * 64 + 64)
                                    ins = nc.tensor.matmul(score[b * S:(b + 1) * S, hp], q1[rows, ts + b * S:ts + b * S + S],
                                                           k1[rows, 2 * t + b].rearrange("p h k -> p (h k)"),
                                                           start=False, stop=True, skip_group_check=True)
                        done(ins, "pe_s")
                    elif kind == "PT":
                        a, t = step[1:]
                        if a == 0:
                            after(pe, "pool_norm", ia, t)
                        else:
                            after(pe, "act_exp", ia, TILES * a + t)
                        for half in range(2):
                            free(half)
                            for j in range(4):
                                jj = 4 * half + j
                                ins = nc.tensor.transpose(turn[:, half, j * P:(j + 1) * P],
                                                          prob[:, t % 2, jj * P:(jj + 1) * P], ident_s[:])
                            done(ins, "pe_pt")
                    elif kind == "PV":
                        a, t = step[1:]
                        if a == 0:
                            after(pe, "act_v", ia, t)
                        elif t == 0:
                            after(pe, "act_v1", ia, a - 1)
                        if a == 0:
                            for half in range(2):
                                free(half)
                                after(pe, "act_pt", ia, 2 * (TILES * a + t) + half)
                                for j in range(4):
                                    for b in range(2):
                                        jj = 4 * half + j
                                        ins = nc.tensor.matmul(turn[:, half, j * P + b * S:j * P + (b + 1) * S],
                                                               v0[:, t % 2, b, jj].rearrange("p c d -> p (c d)"),
                                                               probT[:, jj, b * S:(b + 1) * S], start=True, stop=True)
                                done(ins, "pe_pv0")
                        else:
                            free(0)
                            after(pe, "act_pt", ia, 2 * (TILES * a + t) + 1)
                            for j in range(NC0):
                                for b in range(2):
                                    w = 2 * (D1 + 1)
                                    ins = nc.tensor.matmul(turn[b * S:(b + 1) * S, 0, j * w:(j + 1) * w],
                                                           probT[:, j, b * S:(b + 1) * S],
                                                           v1[:, t, b, j].rearrange("p c d -> p (c d)"), start=True, stop=True)
                            done(ins, "pe_pv1")
                    elif kind == "W":
                        a, t = step[1:]
                        free()
                        if a == 0:
                            after(pe, "act_ot", ia, 2 * t + 1)
                            for j in range(NC0):
                                ins = nc.tensor.matmul(work[:, 0:P], attT[:, j], wo_s[:, j], start=j == 0, stop=j == NC0 - 1)
                        else:
                            after(pe, "act_on", ia, TILES * (a - 1) + t)
                            ins = nc.tensor.matmul(work[:, 0:P], o1T[:], l1w_s[:, 4 * (a - 1) + 3], start=True, stop=True)
                        done(ins, "pe_w")
                    elif kind == "XN":
                        a, t = step[1:]
                        free()
                        after(pe, "dve_xn", ia, TILES * (a - 1) + t)
                        done(nc.tensor.transpose(work[:, 0:P], xn[:, t % 2], ident_s[:]), "pe_xn")
                    elif kind == "ON":
                        a, t = step[1:]
                        free()
                        after(pe, "dve_on", ia, TILES * (a - 1) + t)
                        done(nc.tensor.transpose(work[:, 0:P], o1[:], ident_s[:]), "pe_on")
                    elif kind == "QV":
                        a = step[1]
                        if is_zero(ia) and a == 1:
                            pe.wait_ge(s_l1, 32)
                        after(pe, "act_xn", ia, TILES * a - 1)
                        src = nT if a == 1 else cT1
                        if a == 2:
                            after(pe, "act_cT1", ia, 0)
                        free(0)
                        done(nc.tensor.matmul(pj(step, 0), l1w_s[:, 4 * (a - 1)], nT[:], start=True, stop=True), "pe_qv")
                        free(1)
                        done(nc.tensor.matmul(pj(step, 1), l1w_s[:, 4 * (a - 1) + 1], src[:], start=True, stop=True), "pe_qv")
                        free(2)
                        for t in range(TILES):
                            ins = nc.tensor.matmul(pj(step, 2)[:, t * P:(t + 1) * P], src[:, t * P:(t + 1) * P],
                                                   l1w_s[:, 4 * (a - 1) + 2], start=True, stop=True)
                        done(ins, "pe_qv")
                    elif kind == "B0":
                        free()
                        after(pe, "dve_hn3", ib, 0)
                        for t in range(TILES):
                            ins = nc.tensor.transpose(pj(step, 0)[:, t * P:(t + 1) * P], hn3[:, t], ident_s[:])
                        done(ins, "pe_h3")
                    elif kind == "LG":
                        free()
                        after(pe, "act_h3", ib, 0)
                        for t in range(TILES):
                            ins = nc.tensor.matmul(pj(step, 0)[:, t * E:(t + 1) * E], hn3T[:, t * P:(t + 1) * P], gw_s[:],
                                                   start=True, stop=True)
                        done(ins, "pe_lg")
                    elif kind == "UP":
                        e = step[1]
                        if e == 0:
                            pe.wait_ge(s_w1, 16)
                        for c in range(HC):
                            free(c)
                            done(nc.tensor.matmul(pj(step, c), w1_s[:, HC * e + c], hn3T[:], start=True, stop=True), "pe_up")
                    elif kind == "DN":
                        e = step[1]
                        if e == 0:
                            pe.wait_ge(s_w2, 16)
                            if not is_zero(ib):
                                after(pe, "dve_wt", ib - 1, NE - 1)
                        else:
                            after(pe, "dve_wt", ib, e - 1)
                        after(pe, "dve_hid", ib, HC * e + HC - 1)
                        for t in range(TILES):
                            for c in range(HC):
                                ins = nc.tensor.matmul(down[:, t * P:(t + 1) * P], hid[:, c, t * P:(t + 1) * P],
                                                       w2_s[:, HC * e + c], start=c == 0, stop=c == HC - 1)
                        done(ins, "pe_dn")

            iteration(0, 0, 0, part("C"))
            iteration(0, 0, 1, part("AC"))
            iteration(1, 0, 2, part("ABC"))
            with pe.Fori(2, groups - 1) as i:
                iteration(i, i - 1, i + 1, part("ABC"))
            iteration(groups - 1, groups - 2, groups, part("AB"))
            iteration(groups, groups - 1, groups, part("B"))


def layout(inputs):
    a = {k: np.ascontiguousarray(v) for k, v in inputs.items()}
    tokens = a["x"].shape[0] * S
    c = np.ascontiguousarray

    def rope_columns(w):
        return c(w.reshape(P, 2, NC0, D0 // 2, 2).transpose(0, 2, 1, 4, 3).reshape(P, NC0, P))

    inv_freq = (1.0 / np.float32(10000.0) ** (np.arange(0, D0, 2, dtype=np.float32) / np.float32(D0))).astype(np.float32)
    freqs = (np.arange(S, dtype=np.float32)[None, :] * inv_freq[:, None]).astype(np.float32)
    cos = np.tile(np.cos(freqs), (4, 1)).astype(np.float32)
    sin = np.tile(np.concatenate([np.sin(freqs), -np.sin(freqs)], 0), (2, 1)).astype(np.float32)
    rows = np.arange(P)
    headmask = ((rows % 64) // D1 == np.arange(H // 2)[:, None]).T.astype(np.float32)
    l1 = np.stack([a["L1_xattn_" + n].T for n in ("sa_wq", "sa_wk", "sa_wv", "sa_wo", "ca_wq", "ca_wk", "ca_wv", "ca_wo")], 1)
    w1 = np.concatenate([a["L1_xattn_sh_w1"][None], a["L1_xattn_exp_w1"]], 0)
    w2 = np.concatenate([a["L1_xattn_sh_w2"][None], a["L1_xattn_exp_w2"]], 0)
    return {
        "x": a["x"].reshape(tokens, P), "ctx": a["ctx_1024"].reshape(tokens, P),
        "m0": a["mask_BxS2_bf1"].view(np.uint8), "m1": a["mask_BxSxS_ik0"].reshape(tokens, S),
        "m2": a["mask_BxSxS2_if1"].reshape(tokens, S),
        "wq": rope_columns(a["L0_xattn_Wq"]), "wk": rope_columns(a["L0_xattn_Wk"]), "wv": a["L0_xattn_Wv"],
        "wo": c(a["L0_xattn_Wo"].reshape(NC0, P, P).transpose(1, 0, 2)),
        "gamma": a["L0_xattn_ln_gamma"], "beta": a["L0_xattn_ln_beta"],
        "norms": c(np.stack([a[f"L1_xattn_norm{n}_w"] for n in (1, 2, 3)], 1)),
        "l1w": c(l1), "gw": c(a["L1_xattn_gate_w"].T),
        "w1": c(w1.reshape(NE, HC, P, P).transpose(3, 0, 1, 2).reshape(P, NE * HC, P)),
        "w2": c(w2.reshape(NE, P, HC, P).transpose(3, 0, 2, 1).reshape(P, NE * HC, P)),
        "cos": cos, "sin": sin, "ident": np.eye(P, dtype=np.float32), "headmask": c(headmask),
        "countdown": np.tile(np.arange(E, 0, -1, dtype=np.float32), (P, 1)),
    }


def kernel(**inputs):
    import concourse.bacc as bacc
    from concourse.bass_utils import run_bass_kernel_spmd
    nc = bacc.Bacc("TRN2", target_bir_lowering=False, num_devices=1)
    arrays = {f"in_{k}": v for k, v in layout(inputs).items()}
    aps = [nc.dram_tensor(k, v.shape, mybir.dt.from_np(v.dtype), kind="ExternalInput").ap() for k, v in arrays.items()]
    shape = inputs["x"].shape
    out = nc.dram_tensor("out_y", (shape[0] * shape[1], shape[2]), F32, kind="ExternalOutput").ap()
    build(nc, *aps, out)
    result = run_bass_kernel_spmd(nc, [arrays], core_ids=[0])
    return result.results[0]["out_y"].reshape(shape)
```

```python
import numpy as np
import concourse.bass as bass
from concourse import mybir
from contextlib import ExitStack

F32 = mybir.dt.float32
BF16 = mybir.dt.bfloat16
I32 = mybir.dt.int32
U8 = mybir.dt.uint8
ALU = mybir.AluOpType
ACT = mybir.ActivationFunctionType
AX = mybir.AxisListType

P = 128
S = 64
TILES = 4
G = TILES * P
B = G // S
H = 16
D0 = 64
D1 = 8
NC0 = H * D0 // P
E = 8
NE = E + 1
HC = 4
MASKED = -float(2.0 ** 100)
BIG = 3.0e38


ORDER = {
    "pool": """
    PT-0.0 PT-0.1 PT-0.2 DN-0 PT-0.3 W-0.0 W-0.1 W-0.2 LN-0 LN-1 W-0.3 LN-2 DN-1 LN-3 DN-2 DN-3 QK-1 QK-3
    W-1.0 W-1.1 W-1.2 W-1.3 QK-5 DN-4 DN-5 DN-6 QK-7 QK-9 QK-11 W-2.0 QK-13 DN-7 QK-15 W-2.1 W-2.2 W-2.3 DN-8
    """,
    "act": """
    HN UP-0.0 S-0.0 UP-0.1 UP-0.2 UP-0.3 PT-0.0 V-0 S-0.1 V-1 UP-1.0 UP-1.1 S-0.2 PV-0.0 UP-1.2 UP-1.3 LG V-2
    PT-0.1 S-0.3 UP-2.0 PV-0.1 UP-2.1 UP-2.2 PT-0.2 PV-0.2 V-3 PT-0.3 LD PV-0.3 UP-2.3 XN-1.0 XN-1.1 UP-3.0
    UP-3.1 XN-1.2 UP-3.2 XN-1.3 UP-3.3 QV-1 S-1.0 PT-1.0 S-1.1 UP-4.0 UP-4.1 UP-4.2 PT-1.1 UP-4.3 ON-1.0 S-1.2
    S-1.3 PT-1.2 ON-1.1 UP-5.0 UP-5.1 PT-1.3 ON-1.2 UP-5.2 UP-5.3 XN-2.0 ON-1.3 XN-2.1 UP-6.0 UP-6.1 XN-2.2
    UP-6.2 XN-2.3 UP-6.3 QV-2 UP-7.0 S-2.0 UP-7.1 PT-2.0 UP-7.2 S-2.1 UP-7.3 PT-2.1 ON-2.0 S-2.2 PT-2.2 S-2.3
    ON-2.1 UP-8.0 UP-8.1 PT-2.3 UP-8.2 UP-8.3 ON-2.2 ON-2.3 ST
    """,
    "dve": """
    HN S-0.0 UP-0.0 SM-0 UP-0.1 UP-0.2 UP-0.3 S-0.1 SM-1 S-0.2 UP-1.0 UP-1.1 DN-0 UP-1.2 UP-1.3 LG SM-2 S-0.3
    UP-2.0 SM-3 W-0.0 UP-2.1 UP-2.2 W-0.1 W-0.2 LN-0 LN-1 LN-2 DN-1 UP-2.3 RN-1.0 W-0.3 RN-1.1 LN-3 RN-1.2
    RN-1.3 UP-3.0 UP-3.1 DN-2 UP-3.2 UP-3.3 QV-1 QK-0 QK-1 S-1.0 DN-3 QK-2 QK-3 S-1.1 PV-1.0 UP-4.0 UP-4.1
    S-1.2 PV-1.1 UP-4.2 UP-4.3 S-1.3 QK-4 W-1.0 W-1.1 PV-1.2 UP-5.0 UP-5.1 RN-2.0 DN-4 RN-2.1 UP-5.2 UP-5.3
    W-1.2 PV-1.3 QK-5 QK-6 QK-7 W-1.3 RN-2.2 UP-6.0 RN-2.3 UP-6.1 UP-6.2 UP-6.3 DN-5 QV-2 QK-8 QK-9 S-2.0
    UP-7.0 UP-7.1 S-2.1 UP-7.2 PV-2.0 DN-6 S-2.2 UP-7.3 QK-10 PV-2.1 QK-11 QK-12 W-2.0 S-2.3 QK-13 QK-14
    PV-2.2 W-2.1 QK-15 MB UP-8.0 UP-8.1 DN-7 UP-8.2 UP-8.3 W-2.2 PV-2.3 W-2.3 DN-8
    """,
    "pe": """
    S-0.0 HN UP-0.0 UP-0.1 S-0.1 UP-0.2 UP-0.3 PT-0.0 V-0 DN-0.0 DN-0.1 V-1 S-0.2 UP-1.0 UP-1.1 PV-0.0 UP-1.2
    UP-1.3 PT-0.1 LG V-2 S-0.3 DN-1.0 DN-1.1 UP-2.0 W-0.0 PV-0.1 UP-2.1 UP-2.2 PT-0.2 W-0.1 PV-0.2 V-3 PT-0.3
    W-0.2 LD PV-0.3 UP-2.3 W-0.3 DN-2.0 XN-1.0 UP-3.0 XN-1.1 DN-2.1 UP-3.1 XN-1.2 UP-3.2 XN-1.3 UP-3.3 QV-1
    DN-3.0 QK-0 QK-1 S-1.0 DN-3.1 QK-2 QK-3 S-1.1 PT-1.0 UP-4.0 PV-1.0 UP-4.1 S-1.2 UP-4.2 PT-1.1 UP-4.3
    ON-1.0 PV-1.1 S-1.3 PT-1.2 DN-4.0 QK-4 W-1.0 DN-4.1 ON-1.1 PV-1.2 W-1.1 UP-5.0 UP-5.1 ON-1.2 PT-1.3 UP-5.2
    UP-5.3 W-1.2 PV-1.3 QK-5 QK-6 XN-2.0 DN-5.0 ON-1.3 QK-7 XN-2.1 UP-6.0 W-1.3 DN-5.1 UP-6.1 XN-2.2 UP-6.2
    XN-2.3 UP-6.3 QV-2 QK-8 DN-6.0 QK-9 S-2.0 DN-6.1 UP-7.0 UP-7.1 S-2.1 PT-2.0 UP-7.2 PV-2.0 S-2.2 UP-7.3
    PT-2.1 QK-10 ON-2.0 PV-2.1 QK-11 QK-12 W-2.0 PT-2.2 S-2.3 DN-7.0 ON-2.1 QK-13 QK-14 PV-2.2 W-2.1 QK-15
    DN-7.1 UP-8.0 UP-8.1 PT-2.3 UP-8.2 ON-2.2 UP-8.3 PV-2.3 W-2.2 DN-8.0 ON-2.3 DN-8.1 W-2.3
    """,
}


def steps_of(text):
    steps = []
    for word in text.split():
        kind, _, rest = word.partition("-")
        steps.append((kind,) + tuple(int(v) for v in rest.split(".") if v))
    return steps


STEPS = {engine: steps_of(text) for engine, text in ORDER.items()}


def stage(step):
    return {"HN": "B", "LG": "B", "UP": "B", "DN": "B", "ST": "B", "MB": "C", "LD": "C", "QK": "C"}.get(step[0], "A")


def part(engine, stages):
    return [s for s in STEPS[engine] if stage(s) in stages]


def bank_uses():
    uses, n = {}, 0
    for s in STEPS["pe"]:
        count = {"LD": 2, "QK": 1, "V": 2, "QV": 3, "HN": 1, "LG": 1, "UP": 1}.get(s[0], 0)
        for part_of in range(count):
            uses[(s, part_of)] = f"proj{n % 2}"
            n += 1
        if s[0] in ("W", "XN", "ON"):
            uses[(s, 0)] = "work"
        if s[0] in ("PT", "PV"):
            for half in range(2 if s[0] == "PT" or s[1] == 0 else 1):
                uses[(s, half)] = f"turn{half}"
    assert n % 2 == 0
    return uses


BANK_OF = bank_uses()


def build(nc, x, ctx, m0, m1, m2, wq, wk, wv, wo, gamma, beta, norms, l1w, gw, w1, w2, cos, sin, ident,
          headmask, countdown, out):
    groups = x.shape[0] // G
    xg = x.rearrange("(g t p) d -> g p t d", t=TILES, p=P)
    cg = ctx.rearrange("(g t p) d -> g p t d", t=TILES, p=P)
    og = out.rearrange("(g t p) d -> g p t d", t=TILES, p=P)
    m0g = m0.rearrange("(g t b) k -> g b t k", t=TILES, b=2)
    m1g = m1.rearrange("(g t p) k -> g p t k", t=TILES, p=P)
    m2g = m2.rearrange("(g t p) k -> g p t k", t=TILES, p=P)

    with ExitStack() as stack:
        def sb(name, shape, dt=F32):
            return stack.enter_context(nc.sbuf_tensor(name, shape, dt))

        def sem(name):
            return stack.enter_context(nc.semaphore(name))

        wq_s, wk_s = sb("wq_s", [P, NC0, P]), sb("wk_s", [P, NC0, P])
        wv_s, wo_s = sb("wv_s", [P, H * D0]), sb("wo_s", [P, NC0, P])
        l1w_s = sb("l1w_s", [P, 8, P])
        gw_s = sb("gw_s", [P, E])
        w1_s, w2_s = sb("w1_s", [P, NE * HC, P]), sb("w2_s", [P, NE * HC, P])
        gamma_s, beta_s = sb("gamma_s", [P, P]), sb("beta_s", [P, P])
        norms_s = sb("norms_s", [P, 3])
        cos_s, sin_s = sb("cos_s", [P, S]), sb("sin_s", [P, S])
        ident_s, ident_b = sb("ident_s", [P, P]), sb("ident_b", [P, P], BF16)
        headmask_s = sb("headmask_s", [P, H // 2])
        countdown_s = sb("countdown_s", [P, E])
        halves = sb("halves", [P, 1])
        x_s, c_s = sb("x_s", [P, TILES, P]), sb("c_s", [P, TILES, P])
        residual = sb("residual", [P, TILES, P])
        m0_s = sb("m0_s", [P, TILES, S], U8)
        m1_s, m2_s = sb("m1_s", [P, TILES, S], I32), sb("m2_s", [P, TILES, S], I32)
        bias = sb("bias", [P, 3, TILES, S], BF16)
        xT, cT, cT1 = sb("xT", [P, G]), sb("cT", [P, G]), sb("cT1", [P, G])
        qk = sb("qk", [P, 2 * NC0, G])
        part_s, part_m = sb("part_s", [P, 2, 2, G]), sb("part_m", [P, 2, 2, G])
        v0 = sb("v0", [P, 2, 2, NC0, 2, D0])
        prob = sb("prob", [P, 2, H * S])
        probT = sb("probT", [P, NC0, P])
        attT = sb("attT", [P, NC0, P])
        rowmax, rowsum, rowinv = sb("rowmax", [P, H]), sb("rowsum", [P, H]), sb("rowinv", [P, H])
        nT = sb("nT", [P, G])
        q1 = sb("q1", [P, G])
        k1 = sb("k1", [P, B, H // 2, S])
        v1 = sb("v1", [P, TILES, 2, NC0, 2, D1 + 1])
        inv1 = sb("inv1", [P, H])
        o1, o1T = sb("o1", [P, P]), sb("o1T", [P, P])
        h = sb("h", [P, TILES, P])
        xn = sb("xn", [P, 2, P])
        square, total = sb("square", [P, P]), sb("total", [P, 1])
        var0, rstd0 = sb("var0", [P, TILES]), sb("rstd0", [P, TILES])
        var1, rstd1 = sb("var1", [P, 3, TILES]), sb("rstd1", [P, 3, TILES])
        mean0 = sb("mean0", [P, 1])
        hn3, hn3T = sb("hn3", [P, TILES, P]), sb("hn3T", [P, G])
        hid, tanh = sb("hid", [P, HC, G]), sb("tanh", [P, 2, G])
        acc = sb("acc", [P, TILES, P])
        weighted = sb("weighted", [P, 2, TILES, P])
        lg = sb("lg", [P, TILES, E])
        eq, key = sb("eq", [P, TILES, E]), sb("key", [P, TILES, E])
        first, second, lg2, gates = (sb(n, [P, TILES, E]) for n in ("first", "second", "lg2", "gates"))
        top1, top2, keymax, gap, e2, den, g1, g2 = (
            sb(n, [P, TILES]) for n in ("top1", "top2", "keymax", "gap", "e2", "den", "g1", "g2"))

        proj = stack.enter_context(nc.psum_tensor("proj", [P, 2, 512], F32))
        score = stack.enter_context(nc.psum_tensor("score", [P, 2, 512], F32))
        turn = stack.enter_context(nc.psum_tensor("turn", [P, 2, 512], F32))
        down = stack.enter_context(nc.psum_tensor("down", [P, 512], F32))
        work = stack.enter_context(nc.psum_tensor("work", [P, 512], F32))

        def pj(step, n):
            return proj[:, int(BANK_OF[(step, n)][-1]), :]

        per = {}

        def counted(name, n):
            s = sem(name)
            per[name] = (s, n)
            return name

        for name, n in (
            ("pe_xc", 2), ("pe_qk", 2 * NC0), ("pe_v", TILES), ("pe_s", 3 * TILES), ("pe_pt", 6 * TILES),
            ("pe_pv0", 2 * TILES), ("pe_pv1", 2 * TILES), ("pe_on", 2 * TILES), ("pe_w", 3 * TILES),
            ("pe_xn", 2 * TILES), ("pe_qv", 6), ("pe_h3", 1), ("pe_lg", 1), ("pe_up", NE * HC), ("pe_dn", NE),
            ("act_xc", 2), ("act_v", TILES), ("act_exp", 3 * TILES), ("act_pt", 6 * TILES), ("act_ot", 2 * TILES),
            ("act_on", 2 * TILES), ("act_xn", 2 * TILES), ("act_q1", 2), ("act_v1", 2), ("act_h3", 1),
            ("act_e2", 1), ("act_tanh", NE * HC), ("act_cT1", 1), ("act_k1", 2),
            ("dve_bias", 3), ("dve_cos", 2 * NC0), ("dve_sin", 2 * NC0), ("dve_sub", 3 * TILES),
            ("dve_inv", TILES), ("dve_k1", 2), ("dve_on", 2 * TILES), ("dve_w", 3 * TILES),
            ("dve_var0", TILES), ("dve_var1", 3 * TILES), ("dve_ln", TILES), ("dve_xn", 2 * TILES), ("dve_hn3", 1),
            ("dve_lg", 1), ("dve_hid", NE * HC), ("dve_gap", 1), ("dve_gates", 1), ("dve_wt", NE),
            ("pool_qk", 2 * NC0), ("pool_norm", TILES), ("pool_rstd0", TILES), ("pool_rstd1", 3 * TILES),
            ("pool_acc", NE),
        ):
            counted(name, n)
        s_w0, s_wv, s_w1, s_w2, s_l1 = sem("load_wqk"), sem("load_wv"), sem("load_w1"), sem("load_w2"), sem("load_l1")
        s_tab = sem("load_tables")
        s_x, s_c, s_m, s_res = sem("load_x"), sem("load_ctx"), sem("load_masks"), sem("load_residual")
        s_move = [sem("partners_moved0"), sem("partners_moved1")]
        s_out = sem("stored")
        s_init, s_idb = sem("buffers_initialised"), sem("identity_bf16")
        s_chainA, s_chainB = sem("vector_chain_a"), sem("vector_chain_b")

        def after(eng, name, it, n):
            s, k = per[name]
            eng.wait_ge(s, it * k + (n + 1))

        def done(ins, name):
            ins.then_inc(per[name][0], 1)

        def is_zero(it):
            return isinstance(it, int) and it == 0

        def readers(step, n):
            kind = step[0]
            if kind == "LD":
                return [("act_xc", n)]
            if kind == "QK":
                return [("dve_sin", step[1])]
            if kind == "V":
                return [("act_v", step[1])]
            if kind == "QV":
                g = step[1] - 1
                return ([("act_q1", g)], [("act_k1", g)], [("act_v1", g)])[n]
            if kind == "HN":
                return [("act_h3", 0)]
            if kind == "LG":
                return [("dve_lg", 0)]
            if kind == "UP":
                return [("dve_hid", HC * step[1] + step[2])]
            if kind == "W":
                return [("dve_w", TILES * step[1] + step[2])]
            if kind == "XN":
                return [("act_xn", TILES * (step[1] - 1) + step[2])]
            if kind == "ON":
                return [("act_on", TILES * (step[1] - 1) + step[2])]
            if kind == "PT":
                return [("act_pt", 2 * (TILES * step[1] + step[2]) + n)]
            if kind == "PV":
                return [("act_ot", 2 * step[2] + n) if step[1] == 0 else ("dve_on", TILES * (step[1] - 1) + step[2])]

        def bank_free(pe, steps, step, n, of):
            bank = BANK_OF[(step, n)]
            uses = [(s, m) for s in steps for m in range(HC) if BANK_OF.get((s, m)) == bank]
            at = uses.index((step, n))
            if at:
                s, m = uses[at - 1]
                for name, k in readers(s, m):
                    after(pe, name, of[stage(s)], k)
                return
            for st in "ABC":
                mine = [(s, m) for s in STEPS["pe"] for m in range(HC) if BANK_OF.get((s, m)) == bank and stage(s) == st]
                if mine and not is_zero(of[st]):
                    for name, _ in readers(*mine[-1]):
                        sm, count = per[name]
                        pe.wait_ge(sm, of[st] * count)

        block = stack.enter_context(nc.Block())

        @block.sync
        def _(sp):
            sp.dma_start(cos_s[:], cos).then_inc(s_tab, 16)
            sp.dma_start(sin_s[:], sin).then_inc(s_tab, 16)
            sp.dma_start(ident_s[:], ident).then_inc(s_tab, 16)
            sp.dma_start(headmask_s[:], headmask).then_inc(s_tab, 16)
            sp.dma_start(countdown_s[:], countdown).then_inc(s_tab, 16)
            sp.dma_start(gamma_s[:], gamma.partition_broadcast(P)).then_inc(s_tab, 16)
            sp.dma_start(beta_s[:], beta.partition_broadcast(P)).then_inc(s_tab, 16)
            sp.dma_start(norms_s[:], norms).then_inc(s_tab, 16)

            def iteration(ia, first):
                def released(name, n):
                    if not first:
                        after(sp, name, ia - 1, n)

                released("pe_xc", 1)
                sp.dma_start(x_s[:], xg[ia]).then_inc(s_x, 16)
                sp.dma_start(c_s[:], cg[ia]).then_inc(s_c, 16)
                released("dve_w", TILES - 1)
                sp.dma_start(residual[:], xg[ia]).then_inc(s_res, 16)
                for b in range(2):
                    sp.dma_start(m0_s[b * S:(b + 1) * S], m0g[ia, b].partition_broadcast(S)).then_inc(s_m, 16)
                sp.dma_start(m1_s[:], m1g[ia]).then_inc(s_m, 16)
                sp.dma_start(m2_s[:], m2g[ia]).then_inc(s_m, 16)
                if first:
                    sp.dma_start(wq_s[:], wq).then_inc(s_w0, 16)
                    sp.dma_start(wk_s[:], wk).then_inc(s_w0, 16)
                    sp.dma_start(wv_s[:], wv).then_inc(s_wv, 16)
                    sp.dma_start(wo_s[:], wo).then_inc(s_wv, 16)
                    sp.dma_start(l1w_s[:], l1w).then_inc(s_l1, 16)
                    sp.dma_start(gw_s[:], gw).then_inc(s_l1, 16)
                    sp.dma_start(w1_s[:], w1).then_inc(s_w1, 16)
                    sp.dma_start(w2_s[:], w2).then_inc(s_w2, 16)
                for pair in range(NC0):
                    after(sp, "dve_sin", ia, 2 * pair + 1)
                    r = pair % 2
                    for quad in range(4):
                        to = quad ^ 1
                        sp.dma_start(part_m[32 * to:32 * to + 32, r], part_s[32 * quad:32 * quad + 32, r])\
                          .then_inc(s_move[r], 16)

            iteration(0, True)
            iteration(1, False)
            with sp.Fori(2, groups) as i:
                iteration(i, False)

        @block.gpsimd
        def _(pool):
            nc.gpsimd.memset(halves[:], -0.5).then_inc(s_init, 1)
            nc.gpsimd.memset(v0[:], 0.0).then_inc(s_init, 1)
            nc.gpsimd.memset(v1[:], 0.0).then_inc(s_init, 1)
            pool.wait_ge(s_init, 3)
            for cc in range(2):
                nc.gpsimd.memset(v1[cc * S:(cc + 1) * S, :, :, :, cc, D1:D1 + 1], 1.0).then_inc(s_init, 1)
            pool.wait_ge(s_init, 5)

            def iteration(ia, ib, ic, steps):
                for step in steps:
                    kind = step[0]
                    if kind == "QK" and step[1] % 2:
                        pair = step[1] // 2
                        pool.wait_ge(s_move[pair % 2], 64 * (pair // 2 + 1) + ic * (64 * NC0 // 2))
                        for c in range(2):
                            n = 2 * pair + c
                            done(nc.gpsimd.tensor_tensor(qk[:, n], qk[:, n], part_m[:, pair % 2, c], ALU.add), "pool_qk")
                    elif kind == "PT" and step[1] == 0:
                        t = step[2]
                        after(pool, "dve_inv", ia, t)
                        pr = prob[:, t % 2].rearrange("p (h k) -> p h k", h=H)
                        done(nc.gpsimd.tensor_tensor(pr, pr, rowinv[:].unsqueeze(2).to_broadcast([P, H, S]), ALU.mult),
                             "pool_norm")
                    elif kind == "W":
                        a, t = step[1:]
                        if a == 0:
                            after(pool, "dve_var0", ia, t)
                            done(nc.gpsimd.tensor_tensor(rstd0[:, t:t + 1], var0[:, t:t + 1], halves[:], ALU.pow), "pool_rstd0")
                        else:
                            after(pool, "dve_var1", ia, TILES * a + t)
                            done(nc.gpsimd.tensor_tensor(rstd1[:, a, t:t + 1], var1[:, a, t:t + 1], halves[:], ALU.pow),
                                 "pool_rstd1")
                    elif kind == "LN":
                        t = step[1]
                        after(pool, "dve_var1", ia, t)
                        done(nc.gpsimd.tensor_tensor(rstd1[:, 0, t:t + 1], var1[:, 0, t:t + 1], halves[:], ALU.pow),
                             "pool_rstd1")
                    elif kind == "DN":
                        e = step[1]
                        after(pool, "dve_wt", ib, e)
                        if e == 0:
                            if not is_zero(ib):
                                pool.wait_ge(s_out, ib * 16)
                        else:
                            after(pool, "pool_acc", ib, e - 1)
                        done(nc.gpsimd.tensor_tensor(acc[:], acc[:] if e else h[:], weighted[:, e % 2], ALU.add), "pool_acc")

            iteration(0, 0, 0, part("pool", "C"))
            iteration(0, 0, 1, part("pool", "AC"))
            iteration(1, 0, 2, part("pool", "ABC"))
            with pool.Fori(2, groups - 1) as i:
                iteration(i, i - 1, i + 1, part("pool", "ABC"))
            iteration(groups - 1, groups - 2, groups, part("pool", "AB"))
            iteration(groups, groups - 1, groups, part("pool", "B"))

        @block.scalar
        def _(act):
            def iteration(ia, ib, ic, steps):
                for step in steps:
                    kind = step[0]
                    if kind == "LD":
                        if not is_zero(ic):
                            after(act, "pe_v", ic - 1, TILES - 1)
                        for n, dst in enumerate((xT, cT)):
                            after(act, "pe_xc", ic, n)
                            done(nc.scalar.copy(dst[:], pj(step, n)), "act_xc")
                    elif kind == "V":
                        t = step[1]
                        after(act, "pe_v", ia, t)
                        if is_zero(ia) and t == 0:
                            act.wait_ge(s_init, 5)
                        if t >= 2:
                            after(act, "pe_pv0", ia, 2 * (t - 2) + 1)
                        elif not is_zero(ia):
                            after(act, "pe_pv0", ia - 1, 2 * (t + 2) + 1)
                        for b in range(2):
                            for cc in range(2):
                                src = proj[b * S:(b + 1) * S].rearrange("p n (j c d) -> p (n j) c d", c=2, d=D0)[:, :, cc]
                                ins = nc.scalar.copy(v0[cc * S:(cc + 1) * S, t % 2, b, :, cc], src)
                        done(ins, "act_v")
                        if t == 0:
                            if not is_zero(ia):
                                after(act, "pe_qv", ia - 1, 5)
                            after(act, "act_xc", ia, 1)
                            done(nc.scalar.copy(cT1[:], cT[:]), "act_cT1")
                    elif kind == "S":
                        a, t = step[1:]
                        after(act, "dve_sub", ia, TILES * a + t)
                        done(nc.scalar.activation(prob[:, t % 2], prob[:, t % 2], ACT.Exp,
                                                  scale=float((D1 if a else D0) ** -0.5)), "act_exp")
                    elif kind == "PT":
                        a, t = step[1:]
                        for half in range(2):
                            after(act, "pe_pt", ia, 2 * (TILES * a + t) + half)
                            if a > 1 or a == 1 and t:
                                after(act, "pe_pv1", ia, TILES * (a - 1) + t - 1)
                            elif a or t:
                                after(act, "pe_pv0", ia, 2 * (TILES * a + t - 1) + half)
                            elif not is_zero(ia):
                                after(act, "pe_pv1", ia - 1, 2 * TILES - 1)
                            done(nc.scalar.copy(probT[:, 4 * half:4 * half + 4], turn[:, half, :]), "act_pt")
                    elif kind == "PV" and step[1] == 0:
                        t = step[2]
                        for half in range(2):
                            after(act, "pe_pv0", ia, 2 * t + half)
                            if t:
                                after(act, "pe_w", ia, t - 1)
                            elif not is_zero(ia):
                                after(act, "pe_w", ia - 1, TILES - 1)
                            done(nc.scalar.copy(attT[:, 4 * half:4 * half + 4], turn[:, half, :]), "act_ot")
                    elif kind == "XN":
                        a, t = step[1:]
                        after(act, "pe_xn", ia, TILES * (a - 1) + t)
                        if is_zero(ia) and a == 1 and t == 0:
                            act.wait_ge(s_tab, 8 * 16)
                        done(nc.scalar.mul(nT[:, t * P:(t + 1) * P], work[:, 0:P], norms_s[:, a - 1:a]), "act_xn")
                    elif kind == "QV":
                        a = step[1]
                        after(act, "pe_qv", ia, 3 * (a - 1))
                        done(nc.scalar.copy(q1[:], pj(step, 0)), "act_q1")
                        after(act, "pe_qv", ia, 3 * (a - 1) + 1)
                        done(nc.scalar.copy(k1[:, :, H // 2 - 1], pj(step, 1).rearrange("p (b s) -> p b s", b=B)), "act_k1")
                        after(act, "pe_qv", ia, 3 * (a - 1) + 2)
                        src = pj(step, 2).rearrange("p (t j c d) -> p t j c d", t=TILES, c=2, d=D1)
                        for b in range(2):
                            for cc in range(2):
                                ins = nc.scalar.copy(v1[cc * S:(cc + 1) * S, :, b, :, cc, 0:D1],
                                                     src[b * S:(b + 1) * S, :, :, cc])
                        done(ins, "act_v1")
                    elif kind == "ON":
                        a, t = step[1:]
                        after(act, "pe_on", ia, TILES * (a - 1) + t)
                        if t or a > 1:
                            after(act, "pe_w", ia, TILES * a + t - 1)
                        elif not is_zero(ia):
                            after(act, "pe_w", ia - 1, 3 * TILES - 1)
                        done(nc.scalar.copy(o1T[:], work[:, 0:P]), "act_on")
                    elif kind == "HN":
                        after(act, "pe_h3", ib, 0)
                        done(nc.scalar.mul(hn3T[:], pj(step, 0), norms_s[:, 2:3]), "act_h3")
                    elif kind == "LG":
                        after(act, "dve_gap", ib, 0)
                        done(nc.scalar.activation(e2[:], gap[:], ACT.Exp), "act_e2")
                    elif kind == "UP":
                        e, c = step[1:]
                        after(act, "pe_up", ib, HC * e + c)
                        if HC * e + c >= 2:
                            after(act, "dve_hid", ib, HC * e + c - 2)
                        elif not is_zero(ib):
                            after(act, "dve_hid", ib - 1, HC * NE + c - 2)
                        done(nc.scalar.activation(tanh[:, c % 2], pj(step, 0), ACT.Tanh, scale=0.5), "act_tanh")
                    elif kind == "ST":
                        after(act, "pool_acc", ib, NE - 1)
                        act.dma_start(og[ib], acc[:]).then_inc(s_out, 16)

            iteration(0, 0, 0, part("act", "C"))
            iteration(0, 0, 1, part("act", "AC"))
            iteration(1, 0, 2, part("act", "ABC"))
            with act.Fori(2, groups - 1) as i:
                iteration(i, i - 1, i + 1, part("act", "ABC"))
            iteration(groups - 1, groups - 2, groups, part("act", "AB"))
            iteration(groups, groups - 1, groups, part("act", "B"))
            act.wait_ge(s_out, groups * 16)

        LINKS_A, LINKS_B = 58, 18

        @block.vector
        def _(dve):
            dve.wait_ge(s_tab, 8 * 16)
            nc.vector.tensor_copy(ident_b[:], ident_s[:]).then_inc(s_idb, 1)

            def iteration(ia, ib, ic, steps):
                links = {"A": 0, "B": 0}

                def link(ins, which="A"):
                    s, it, k = (s_chainA, ia, LINKS_A) if which == "A" else (s_chainB, ib, LINKS_B)
                    links[which] += 1
                    ins.then_inc(s, 1)
                    dve.wait_ge(s, it * k + links[which])

                def mean_square(src, dst, a, t):
                    link(nc.vector.tensor_tensor_reduce(out=square[:], in0=src, in1=src, scale=1.0, scalar=0.0,
                                                        op0=ALU.mult, op1=ALU.add, accum_out=total[:]))
                    done(nc.vector.tensor_scalar(dst, total[:], 1.0 / P, 1e-5, ALU.mult, ALU.add), "dve_var1")

                for step in steps:
                    kind = step[0]
                    if kind == "MB":
                        dve.wait_ge(s_m, 64 * (ic + 1))
                        if not is_zero(ic):
                            after(dve, "pe_s", ic - 1, 3 * TILES - 1)
                        for n, m in enumerate((m0_s, m1_s, m2_s)):
                            done(nc.vector.tensor_scalar(bias[:, n], m[:], 0.0, MASKED, ALU.is_equal, ALU.mult), "dve_bias")
                    elif kind == "QK":
                        n = step[1]
                        after(dve, "pe_qk", ic, n)
                        pair = n // 2
                        if not is_zero(ic):
                            after(dve, "pe_s", ic - 1, TILES - 1)
                        src = pj(step, 0).rearrange("p (b s) -> p b s", b=B)
                        tab = [tb[:].unsqueeze(1).to_broadcast([P, B, S]) for tb in (cos_s, sin_s)]
                        done(nc.vector.tensor_tensor(qk[:, n].rearrange("p (b s) -> p b s", b=B), src, tab[0], ALU.mult),
                             "dve_cos")
                        if pair >= 2:
                            after(dve, "pool_qk", ic, 2 * (pair - 2) + 1)
                        elif not is_zero(ic):
                            after(dve, "pool_qk", ic - 1, 2 * (pair + NC0 - 2) + 1)
                        done(nc.vector.tensor_tensor(part_s[:, pair % 2, n % 2].rearrange("p (b s) -> p b s", b=B),
                                                     src, tab[1], ALU.mult), "dve_sin")
                    elif kind == "S":
                        a, t = step[1:]
                        after(dve, "pe_s", ia, TILES * a + t)
                        sc = score[:].rearrange("p n (h k) -> p (n h) k", k=S)
                        pr = prob[:, t % 2].rearrange("p (h k) -> p h k", h=H)
                        link(nc.vector.tensor_reduce(rowmax[:], sc, AX.X, ALU.max))
                        if a or t >= 2:
                            after(dve, "pe_pt", ia, 2 * (TILES * a + t - 2) + 1)
                        elif not is_zero(ia):
                            after(dve, "pe_pt", ia - 1, 2 * (3 * TILES + t - 2) + 1)
                        done(nc.vector.tensor_tensor(pr, sc, rowmax[:].unsqueeze(2).to_broadcast([P, H, S]), ALU.subtract),
                             "dve_sub")
                    elif kind == "SM":
                        t = step[1]
                        after(dve, "act_exp", ia, t)
                        if t:
                            after(dve, "dve_inv", ia, t - 1)
                        elif not is_zero(ia):
                            after(dve, "dve_inv", ia - 1, TILES - 1)
                        link(nc.vector.tensor_reduce(rowsum[:], prob[:, t % 2].rearrange("p (h k) -> p h k", h=H), AX.X, ALU.add))
                        if t:
                            after(dve, "pool_norm", ia, t - 1)
                        elif not is_zero(ia):
                            after(dve, "pool_norm", ia - 1, TILES - 1)
                        done(nc.vector.reciprocal(rowinv[:], rowsum[:]), "dve_inv")
                    elif kind == "W":
                        a, t = step[1:]
                        after(dve, "pe_w", ia, TILES * a + t)
                        ht = h[:, t]
                        if a == 0:
                            if t == 0:
                                dve.wait_ge(s_res, 16 * (ia + 1))
                            if t == 0 and not is_zero(ia):
                                after(dve, "pool_acc", ib, 0)
                            done(nc.vector.tensor_tensor(ht, residual[:, t], work[:, 0:P], ALU.add), "dve_w")
                            after(dve, "dve_w", ia, t)
                            link(nc.vector.tensor_reduce(total[:], ht, AX.X, ALU.add))
                            link(nc.vector.tensor_scalar(mean0[:], total[:], 1.0 / P, None, ALU.mult))
                            link(nc.vector.tensor_scalar(ht, ht, mean0[:], None, ALU.subtract))
                            link(nc.vector.tensor_tensor_reduce(out=square[:], in0=ht, in1=ht, scale=1.0, scalar=0.0,
                                                                op0=ALU.mult, op1=ALU.add, accum_out=total[:]))
                            done(nc.vector.tensor_scalar(var0[:, t:t + 1], total[:], 1.0 / P, 1e-3, ALU.mult, ALU.add),
                                 "dve_var0")
                        else:
                            done(nc.vector.tensor_tensor(ht, ht, work[:, 0:P], ALU.add), "dve_w")
                            after(dve, "dve_w", ia, TILES * a + t)
                            mean_square(ht, var1[:, a, t:t + 1], a, t)
                    elif kind == "LN":
                        t = step[1]
                        ht = h[:, t]
                        after(dve, "pool_rstd0", ia, t)
                        link(nc.vector.scalar_tensor_tensor(out=ht, in0=ht, scalar=rstd0[:, t:t + 1], in1=gamma_s[:],
                                                            op0=ALU.mult, op1=ALU.mult))
                        done(nc.vector.tensor_tensor(ht, ht, beta_s[:], ALU.add), "dve_ln")
                        after(dve, "dve_ln", ia, t)
                        mean_square(ht, var1[:, 0, t:t + 1], 0, t)
                    elif kind == "RN":
                        a, t = step[1:]
                        after(dve, "pool_rstd1", ia, TILES * (a - 1) + t)
                        if t >= 2:
                            after(dve, "pe_xn", ia, TILES * (a - 1) + t - 2)
                        done(nc.vector.tensor_scalar(xn[:, t % 2], h[:, t], rstd1[:, a - 1, t:t + 1], None, ALU.mult),
                             "dve_xn")
                    elif kind == "QV":
                        a = step[1]
                        after(dve, "act_k1", ia, a - 1)
                        kp = k1[:, :, H // 2 - 1]
                        for hh in range(H // 2):
                            if hh == H // 2 - 1:
                                link(ins)
                            ins = nc.vector.tensor_scalar(k1[:, :, hh], kp, headmask_s[:, hh:hh + 1], None, ALU.mult)
                        done(ins, "dve_k1")
                    elif kind == "PV" and step[1]:
                        a, t = step[1:]
                        after(dve, "pe_pv1", ia, TILES * (a - 1) + t)
                        o = turn[:, 0, 0:H * (D1 + 1)].rearrange("p (h d) -> p h d", h=H)
                        link(nc.vector.reciprocal(inv1[:], o[:, :, D1]))
                        if t or a > 1:
                            after(dve, "pe_on", ia, TILES * (a - 1) + t - 1)
                        elif not is_zero(ia):
                            after(dve, "pe_on", ia - 1, 2 * TILES - 1)
                        done(nc.vector.tensor_tensor(o1[:].rearrange("p (h d) -> p h d", h=H), o[:, :, 0:D1],
                                                     inv1[:].unsqueeze(2).to_broadcast([P, H, D1]), ALU.mult), "dve_on")
                    elif kind == "HN":
                        after(dve, "pool_rstd1", ib, 3 * TILES - 1)
                        for t in range(TILES):
                            ins = nc.vector.tensor_scalar(hn3[:, t], h[:, t], rstd1[:, 2, t:t + 1], None, ALU.mult)
                        done(ins, "dve_hn3")
                    elif kind == "LG":
                        def wide(v):
                            return v[:].unsqueeze(2).to_broadcast([P, TILES, E])
                        cd = countdown_s[:].unsqueeze(1).to_broadcast([P, TILES, E])
                        after(dve, "pe_lg", ib, 0)
                        done(nc.vector.tensor_copy(lg[:], pj(step, 0)[:, 0:TILES * E].rearrange("p (t e) -> p t e", e=E)), "dve_lg")
                        after(dve, "dve_lg", ib, 0)
                        for src, top, pick in ((lg, top1, first_of["first"]), (lg2, top2, first_of["second"])):
                            link(nc.vector.tensor_reduce(top[:], src[:], AX.X, ALU.max), "B")
                            link(nc.vector.tensor_tensor(eq[:], src[:], wide(top), ALU.is_equal), "B")
                            link(nc.vector.tensor_tensor(key[:], eq[:], cd, ALU.mult), "B")
                            link(nc.vector.tensor_reduce(keymax[:], key[:], AX.X, ALU.max), "B")
                            link(nc.vector.tensor_tensor(pick[:], key[:], wide(keymax), ALU.is_equal), "B")
                            if src is lg:
                                link(nc.vector.tensor_scalar(lg2[:], pick[:], -BIG, None, ALU.mult), "B")
                                link(nc.vector.tensor_tensor(lg2[:], lg2[:], lg[:], ALU.add), "B")
                        done(nc.vector.tensor_tensor(gap[:], top2[:], top1[:], ALU.subtract), "dve_gap")
                        after(dve, "act_e2", ib, 0)
                        link(nc.vector.tensor_scalar_add(den[:], e2[:], 1.0), "B")
                        link(nc.vector.reciprocal(g1[:], den[:]), "B")
                        link(nc.vector.tensor_scalar(g1[:], g1[:], 0.5, None, ALU.mult), "B")
                        link(nc.vector.tensor_tensor(g2[:], e2[:], g1[:], ALU.mult), "B")
                        link(nc.vector.tensor_tensor(gates[:], first_of["first"][:], wide(g1), ALU.mult), "B")
                        link(nc.vector.tensor_tensor(key[:], first_of["second"][:], wide(g2), ALU.mult), "B")
                        done(nc.vector.tensor_tensor(gates[:], gates[:], key[:], ALU.add), "dve_gates")
                    elif kind == "UP":
                        e, c = step[1:]
                        if e:
                            after(dve, "pe_dn", ib, e - 1)
                        elif not is_zero(ib):
                            after(dve, "pe_dn", ib - 1, NE - 1)
                        after(dve, "act_tanh", ib, HC * e + c)
                        done(nc.vector.scalar_tensor_tensor(out=hid[:, c], in0=tanh[:, c % 2], scalar=1.0, in1=pj(step, 0),
                                                            op0=ALU.add, op1=ALU.mult), "dve_hid")
                    elif kind == "DN":
                        e = step[1]
                        after(dve, "pe_dn", ib, e)
                        if e >= 2:
                            after(dve, "pool_acc", ib, e - 2)
                        elif not is_zero(ib):
                            after(dve, "pool_acc", ib - 1, NE + e - 2)
                        src = down[:].rearrange("p (t d) -> p t d", t=TILES)
                        if e == 0:
                            done(nc.vector.tensor_scalar(weighted[:, 0], src, 0.5, None, ALU.mult), "dve_wt")
                        else:
                            if e == 1:
                                after(dve, "dve_gates", ib, 0)
                            done(nc.vector.tensor_tensor(weighted[:, e % 2], src,
                                                         gates[:, :, e - 1:e].to_broadcast([P, TILES, P]), ALU.mult), "dve_wt")
                assert links["A"] in (0, LINKS_A) and links["B"] in (0, LINKS_B), links

            first_of = {"first": first, "second": second}
            iteration(0, 0, 0, part("dve", "C"))
            iteration(0, 0, 1, part("dve", "AC"))
            iteration(1, 0, 2, part("dve", "ABC"))
            with dve.Fori(2, groups - 1) as i:
                iteration(i, i - 1, i + 1, part("dve", "ABC"))
            iteration(groups - 1, groups - 2, groups, part("dve", "AB"))
            iteration(groups, groups - 1, groups, part("dve", "B"))

        @block.tensor
        def _(pe):
            def iteration(ia, ib, ic, steps):
                for step in steps:
                    kind = step[0]

                    def free(n=0):
                        bank_free(pe, steps, step, n, {"A": ia, "B": ib, "C": ic})

                    if kind == "LD":
                        for n, (src, s) in enumerate(((x_s, s_x), (c_s, s_c))):
                            if is_zero(ic):
                                pe.wait_ge(s_tab, 8 * 16)
                            pe.wait_ge(s, 16 * (ic + 1))
                            free(n)
                            for t in range(TILES):
                                ins = nc.tensor.transpose(pj(step, n)[:, t * P:(t + 1) * P], src[:, t], ident_s[:])
                            done(ins, "pe_xc")
                    elif kind == "QK":
                        n = step[1]
                        free()
                        if n == 0:
                            after(pe, "act_xc", ic, 1)
                            if is_zero(ic):
                                pe.wait_ge(s_w0, 32)
                        w, src = (wq_s, xT) if n < NC0 else (wk_s, cT)
                        done(nc.tensor.matmul(pj(step, 0), w[:, n % NC0], src[:], start=True, stop=True), "pe_qk")
                    elif kind == "V":
                        t = step[1]
                        if is_zero(ia) and t == 0:
                            pe.wait_ge(s_wv, 32)
                        for n in range(2):
                            free(n)
                            half = int(BANK_OF[(step, n)][-1])
                            ins = nc.tensor.matmul(pj(step, n), cT[:, t * P:(t + 1) * P],
                                                   wv_s[:, half * 512:(half + 1) * 512], start=True, stop=True)
                        done(ins, "pe_v")
                    elif kind == "S":
                        a, t = step[1:]
                        if a or t:
                            after(pe, "dve_sub", ia, TILES * a + t - 1)
                        elif not is_zero(ia):
                            after(pe, "dve_sub", ia - 1, 3 * TILES - 1)
                        if t == 0:
                            if a == 0:
                                after(pe, "dve_bias", ia, 2)
                                after(pe, "pool_qk", ia, 2 * NC0 - 1)
                                if is_zero(ia):
                                    pe.wait_ge(s_idb, 1)
                            else:
                                after(pe, "act_q1", ia, a - 1)
                                after(pe, "dve_k1", ia, a - 1)
                        for hp in range(2):
                            nc.tensor.matmul(score[:, hp].rearrange("p (h k) -> p h k", k=S), ident_b[:],
                                             bias[:, a, t].unsqueeze(1).to_broadcast([P, H // 2, S]), start=True, stop=True)
                        ts = t * P
                        if a == 0:
                            for c in range(NC0):
                                for hp in range(2):
                                    for b in range(2):
                                        rows = slice(hp * D0, hp * D0 + D0)
                                        tok = slice(ts + b * S, ts + b * S + S)
                                        ins = nc.tensor.matmul(score[b * S:(b + 1) * S, hp, c * S:(c + 1) * S],
                                                               qk[rows, c, tok], qk[rows, NC0 + c, tok],
                                                               start=False, stop=True, skip_group_check=True)
                        else:
                            for b in range(2):
                                for hp in range(2):
                                    rows = slice(hp * 64, hp * 64 + 64)
                                    ins = nc.tensor.matmul(score[b * S:(b + 1) * S, hp], q1[rows, ts + b * S:ts + b * S + S],
                                                           k1[rows, 2 * t + b].rearrange("p h k -> p (h k)"),
                                                           start=False, stop=True, skip_group_check=True)
                        done(ins, "pe_s")
                    elif kind == "PT":
                        a, t = step[1:]
                        if a == 0:
                            after(pe, "pool_norm", ia, t)
                        else:
                            after(pe, "act_exp", ia, TILES * a + t)
                        for half in range(2):
                            free(half)
                            for j in range(4):
                                jj = 4 * half + j
                                ins = nc.tensor.transpose(turn[:, half, j * P:(j + 1) * P],
                                                          prob[:, t % 2, jj * P:(jj + 1) * P], ident_s[:])
                            done(ins, "pe_pt")
                    elif kind == "PV":
                        a, t = step[1:]
                        if a == 0:
                            after(pe, "act_v", ia, t)
                        elif t == 0:
                            after(pe, "act_v1", ia, a - 1)
                        if a == 0:
                            for half in range(2):
                                free(half)
                                after(pe, "act_pt", ia, 2 * (TILES * a + t) + half)
                                for j in range(4):
                                    for b in range(2):
                                        jj = 4 * half + j
                                        ins = nc.tensor.matmul(turn[:, half, j * P + b * S:j * P + (b + 1) * S],
                                                               v0[:, t % 2, b, jj].rearrange("p c d -> p (c d)"),
                                                               probT[:, jj, b * S:(b + 1) * S], start=True, stop=True)
                                done(ins, "pe_pv0")
                        else:
                            free(0)
                            after(pe, "act_pt", ia, 2 * (TILES * a + t) + 1)
                            for j in range(NC0):
                                for b in range(2):
                                    w = 2 * (D1 + 1)
                                    ins = nc.tensor.matmul(turn[b * S:(b + 1) * S, 0, j * w:(j + 1) * w],
                                                           probT[:, j, b * S:(b + 1) * S],
                                                           v1[:, t, b, j].rearrange("p c d -> p (c d)"), start=True, stop=True)
                            done(ins, "pe_pv1")
                    elif kind == "W":
                        a, t = step[1:]
                        free()
                        if a == 0:
                            after(pe, "act_ot", ia, 2 * t + 1)
                            for j in range(NC0):
                                ins = nc.tensor.matmul(work[:, 0:P], attT[:, j], wo_s[:, j], start=j == 0, stop=j == NC0 - 1)
                        else:
                            after(pe, "act_on", ia, TILES * (a - 1) + t)
                            ins = nc.tensor.matmul(work[:, 0:P], o1T[:], l1w_s[:, 4 * (a - 1) + 3], start=True, stop=True)
                        done(ins, "pe_w")
                    elif kind == "XN":
                        a, t = step[1:]
                        free()
                        after(pe, "dve_xn", ia, TILES * (a - 1) + t)
                        done(nc.tensor.transpose(work[:, 0:P], xn[:, t % 2], ident_s[:]), "pe_xn")
                    elif kind == "ON":
                        a, t = step[1:]
                        free()
                        after(pe, "dve_on", ia, TILES * (a - 1) + t)
                        done(nc.tensor.transpose(work[:, 0:P], o1[:], ident_s[:]), "pe_on")
                    elif kind == "QV":
                        a = step[1]
                        if is_zero(ia) and a == 1:
                            pe.wait_ge(s_l1, 32)
                        after(pe, "act_xn", ia, TILES * a - 1)
                        src = nT if a == 1 else cT1
                        if a == 2:
                            after(pe, "act_cT1", ia, 0)
                        free(0)
                        done(nc.tensor.matmul(pj(step, 0), l1w_s[:, 4 * (a - 1)], nT[:], start=True, stop=True), "pe_qv")
                        free(1)
                        done(nc.tensor.matmul(pj(step, 1), l1w_s[:, 4 * (a - 1) + 1], src[:], start=True, stop=True), "pe_qv")
                        free(2)
                        for t in range(TILES):
                            ins = nc.tensor.matmul(pj(step, 2)[:, t * P:(t + 1) * P], src[:, t * P:(t + 1) * P],
                                                   l1w_s[:, 4 * (a - 1) + 2], start=True, stop=True)
                        done(ins, "pe_qv")
                    elif kind == "HN":
                        free()
                        after(pe, "dve_hn3", ib, 0)
                        for t in range(TILES):
                            ins = nc.tensor.transpose(pj(step, 0)[:, t * P:(t + 1) * P], hn3[:, t], ident_s[:])
                        done(ins, "pe_h3")
                    elif kind == "LG":
                        free()
                        after(pe, "act_h3", ib, 0)
                        for t in range(TILES):
                            ins = nc.tensor.matmul(pj(step, 0)[:, t * E:(t + 1) * E], hn3T[:, t * P:(t + 1) * P], gw_s[:],
                                                   start=True, stop=True)
                        done(ins, "pe_lg")
                    elif kind == "UP":
                        e, c = step[1:]
                        if e == 0 and c == 0:
                            pe.wait_ge(s_w1, 16)
                            after(pe, "act_h3", ib, 0)
                        free()
                        done(nc.tensor.matmul(pj(step, 0), w1_s[:, HC * e + c], hn3T[:], start=True, stop=True), "pe_up")
                    elif kind == "DN":
                        e, half = step[1:]
                        if half:
                            pass
                        elif e == 0:
                            pe.wait_ge(s_w2, 16)
                            if not is_zero(ib):
                                after(pe, "dve_wt", ib - 1, NE - 1)
                        else:
                            after(pe, "dve_wt", ib, e - 1)
                        if not half:
                            after(pe, "dve_hid", ib, HC * e + HC - 1)
                        for t in (2 * half, 2 * half + 1):
                            for c in range(HC):
                                ins = nc.tensor.matmul(down[:, t * P:(t + 1) * P], hid[:, c, t * P:(t + 1) * P],
                                                       w2_s[:, HC * e + c], start=c == 0, stop=c == HC - 1)
                        if half:
                            done(ins, "pe_dn")

            iteration(0, 0, 0, part("pe", "C"))
            iteration(0, 0, 1, part("pe", "AC"))
            iteration(1, 0, 2, part("pe", "ABC"))
            with pe.Fori(2, groups - 1) as i:
                iteration(i, i - 1, i + 1, part("pe", "ABC"))
            iteration(groups - 1, groups - 2, groups, part("pe", "AB"))
            iteration(groups, groups - 1, groups, part("pe", "B"))


def layout(inputs):
    a = {k: np.ascontiguousarray(v) for k, v in inputs.items()}
    tokens = a["x"].shape[0] * S
    c = np.ascontiguousarray

    def rope_columns(w):
        return c(w.reshape(P, 2, NC0, D0 // 2, 2).transpose(0, 2, 1, 4, 3).reshape(P, NC0, P))

    inv_freq = (1.0 / np.float32(10000.0) ** (np.arange(0, D0, 2, dtype=np.float32) / np.float32(D0))).astype(np.float32)
    freqs = (np.arange(S, dtype=np.float32)[None, :] * inv_freq[:, None]).astype(np.float32)
    cos = np.tile(np.cos(freqs), (4, 1)).astype(np.float32)
    sin = np.tile(np.concatenate([np.sin(freqs), -np.sin(freqs)], 0), (2, 1)).astype(np.float32)
    rows = np.arange(P)
    headmask = ((rows % 64) // D1 == np.arange(H // 2)[:, None]).T.astype(np.float32)
    l1 = np.stack([a["L1_xattn_" + n].T for n in ("sa_wq", "sa_wk", "sa_wv", "sa_wo", "ca_wq", "ca_wk", "ca_wv", "ca_wo")], 1)
    w1 = np.concatenate([a["L1_xattn_sh_w1"][None], a["L1_xattn_exp_w1"]], 0)
    w2 = np.concatenate([a["L1_xattn_sh_w2"][None], a["L1_xattn_exp_w2"]], 0)
    return {
        "x": a["x"].reshape(tokens, P), "ctx": a["ctx_1024"].reshape(tokens, P),
        "m0": a["mask_BxS2_bf1"].view(np.uint8), "m1": a["mask_BxSxS_ik0"].reshape(tokens, S),
        "m2": a["mask_BxSxS2_if1"].reshape(tokens, S),
        "wq": rope_columns(a["L0_xattn_Wq"]), "wk": rope_columns(a["L0_xattn_Wk"]), "wv": a["L0_xattn_Wv"],
        "wo": c(a["L0_xattn_Wo"].reshape(NC0, P, P).transpose(1, 0, 2)),
        "gamma": a["L0_xattn_ln_gamma"], "beta": a["L0_xattn_ln_beta"],
        "norms": c(np.stack([a[f"L1_xattn_norm{n}_w"] for n in (1, 2, 3)], 1)),
        "l1w": c(l1), "gw": c(a["L1_xattn_gate_w"].T),
        "w1": c(w1.reshape(NE, HC, P, P).transpose(3, 0, 1, 2).reshape(P, NE * HC, P)),
        "w2": c(w2.reshape(NE, P, HC, P).transpose(3, 0, 2, 1).reshape(P, NE * HC, P)),
        "cos": cos, "sin": sin, "ident": np.eye(P, dtype=np.float32), "headmask": c(headmask),
        "countdown": np.tile(np.arange(E, 0, -1, dtype=np.float32), (P, 1)),
    }


def kernel(**inputs):
    import concourse.bacc as bacc
    from concourse.bass_utils import run_bass_kernel_spmd
    nc = bacc.Bacc("TRN2", target_bir_lowering=False, num_devices=1)
    arrays = {f"in_{k}": v for k, v in layout(inputs).items()}
    aps = [nc.dram_tensor(k, v.shape, mybir.dt.from_np(v.dtype), kind="ExternalInput").ap() for k, v in arrays.items()]
    shape = inputs["x"].shape
    out = nc.dram_tensor("out_y", (shape[0] * shape[1], shape[2]), F32, kind="ExternalOutput").ap()
    build(nc, *aps, out)
    result = run_bass_kernel_spmd(nc, [arrays], core_ids=[0])
    return result.results[0]["out_y"].reshape(shape)
```

```python
import numpy as np
import concourse.bass as bass
from concourse import mybir
from contextlib import ExitStack

F32 = mybir.dt.float32
BF16 = mybir.dt.bfloat16
F32R = mybir.dt.float32r
I32 = mybir.dt.int32
U8 = mybir.dt.uint8
ALU = mybir.AluOpType
ACT = mybir.ActivationFunctionType
AX = mybir.AxisListType

P = 128
S = 64
TILES = 4
G = TILES * P
B = G // S
H = 16
D0 = 64
D1 = 8
NC0 = H * D0 // P
E = 8
NE = E + 1
HC = 4
SPLIT = 6
MASKED = -float(2.0 ** 100)
BIG = 3.0e38


ORDER = {
    "pool": """
    PT-0.0 PT-0.1 PT-0.2 PT-0.3 DN-0 W-0.0 LN-0 W-0.1 W-0.2 DN-1 W-0.3 LN-1 LN-2 LN-3 QK-0 QK-1 DN-2 DN-3 QK-2
    W-1.0 QK-3 W-1.1 DN-4 DN-5 QK-4 QK-5 W-1.2 QK-6 DN-6 W-1.3 QK-7 QK-8 QK-9 QK-10 QK-11 QK-12 DN-7 QK-13
    QK-14 W-2.0 W-2.1 QK-15 W-2.2 DN-8 W-2.3
    """,
    "act": """
    HN S-0.0 V-0 V-1 PT-0.0 S-0.1 UP-0.0 PV-0.0 LG UP-0.1 UP-0.2 UP-0.3 PT-0.1 S-0.2 S-0.3 UP-1.0 UP-1.1
    PV-0.1 UP-1.2 UP-1.3 PT-0.2 V-2 UP-2.0 UP-2.1 UP-2.2 PV-0.2 V-3 PT-0.3 UP-2.3 XN-1.0 PV-0.3 LD UP-3.0
    XN-1.1 UP-3.1 XN-1.2 UP-3.2 XN-1.3 UP-3.3 QV-1 S-1.0 UP-4.0 PT-1.0 UP-4.1 UP-4.2 S-1.1 UP-4.3 UP-5.0
    UP-5.1 ON-1.0 S-1.2 UP-5.2 UP-5.3 PT-1.1 S-1.3 ON-1.1 UP-6.0 UP-6.1 PT-1.2 UP-6.2 UP-6.3 ON-1.2 PT-1.3
    UP-7.0 XN-2.0 UP-7.1 XN-2.1 ON-1.3 UP-7.2 XN-2.2 UP-7.3 XN-2.3 QV-2 UP-8.0 S-2.0 PT-2.0 S-2.1 UP-8.1
    ON-2.0 PT-2.1 S-2.2 PT-2.2 ON-2.1 UP-8.2 UP-8.3 S-2.3 PT-2.3 ON-2.2 ON-2.3 ST
    """,
    "dve": """
    HN S-0.0 SM-0 S-0.1 HS S-0.2 SM-1 UP-0.0 LG UP-0.1 UP-0.2 UP-0.3 S-0.3 SM-2 SM-3 DN-0 UP-1.0 UP-1.1 UP-1.2
    UP-1.3 W-0.0 UP-2.0 LN-0 W-0.1 UP-2.1 UP-2.2 DN-1 RN-1.0 W-0.2 LN-1 UP-2.3 LN-2 W-0.3 LN-3 RN-1.1 RN-1.2
    RN-1.3 UP-3.0 UP-3.1 UP-3.2 UP-3.3 DN-2 QV-1 QK-0 QK-1 S-1.0 QK-2 UP-4.0 S-1.1 UP-4.1 UP-4.2 UP-4.3 DN-3
    PV-1.0 S-1.2 QK-3 DN-4 UP-5.0 UP-5.1 UP-5.2 UP-5.3 W-1.0 QK-4 RN-2.0 PV-1.1 S-1.3 UP-6.0 UP-6.1 W-1.1
    UP-6.2 UP-6.3 PV-1.2 QK-5 RN-2.1 DN-5 W-1.2 QK-6 QK-7 DN-6 UP-7.0 UP-7.1 PV-1.3 RN-2.2 QK-8 W-1.3 RN-2.3
    UP-7.2 UP-7.3 QV-2 QK-9 QK-10 S-2.0 UP-8.0 QK-11 DN-7 S-2.1 QK-12 PV-2.0 QK-13 S-2.2 QK-14 UP-8.1 PV-2.1
    W-2.0 S-2.3 UP-8.2 UP-8.3 PV-2.2 QK-15 W-2.1 MB W-2.2 PV-2.3 DN-8 W-2.3
    """,
    "pe": """
    S-0.0 HN V-0 S-0.1 V-1 PT-0.0 S-0.2 PV-0.0 UP-0.0 LG S-0.3 UP-0.1 UP-0.2 PT-0.1 UP-0.3 W-0.0 UP-1.0 UP-1.1
    DN-0.0 DN-0.1 PV-0.1 UP-1.2 UP-1.3 PT-0.2 V-2 DN-1.0 DN-1.1 UP-2.0 UP-2.1 W-0.1 UP-2.2 PV-0.2 V-3 W-0.2
    PT-0.3 UP-2.3 XN-1.0 PV-0.3 LD W-0.3 UP-3.0 DN-2.0 DN-2.1 XN-1.1 UP-3.1 XN-1.2 UP-3.2 XN-1.3 UP-3.3 QV-1
    DN-3.0 QK-0 QK-1 S-1.0 QK-2 DN-3.1 UP-4.0 S-1.1 PT-1.0 UP-4.1 UP-4.2 PV-1.0 UP-4.3 S-1.2 QK-3 DN-4.0
    DN-4.1 UP-5.0 UP-5.1 ON-1.0 S-1.3 UP-5.2 UP-5.3 W-1.0 PT-1.1 QK-4 PV-1.1 DN-5.0 UP-6.0 DN-5.1 ON-1.1
    UP-6.1 PT-1.2 W-1.1 UP-6.2 UP-6.3 PV-1.2 QK-5 QK-6 ON-1.2 PT-1.3 W-1.2 QK-7 DN-6.0 DN-6.1 UP-7.0 XN-2.0
    UP-7.1 PV-1.3 XN-2.1 QK-8 ON-1.3 W-1.3 UP-7.2 XN-2.2 UP-7.3 XN-2.3 QV-2 DN-7.0 QK-9 QK-10 S-2.0 QK-11
    UP-8.0 DN-7.1 S-2.1 PT-2.0 QK-12 PV-2.0 QK-13 S-2.2 UP-8.1 ON-2.0 PT-2.1 QK-14 W-2.0 PV-2.1 S-2.3 PT-2.2
    ON-2.1 UP-8.2 UP-8.3 PV-2.2 QK-15 PT-2.3 W-2.1 DN-8.0 ON-2.2 PV-2.3 W-2.2 DN-8.1 ON-2.3 W-2.3
    """,
}


def steps_of(text):
    steps = []
    for word in text.split():
        kind, _, rest = word.partition("-")
        steps.append((kind,) + tuple(int(v) for v in rest.split(".") if v))
    return steps


STEPS = {engine: steps_of(text) for engine, text in ORDER.items()}


def stage(step):
    return {"HN": "B", "HS": "B", "LG": "B", "UP": "B", "DN": "B", "ST": "B", "MB": "C", "LD": "C", "QK": "C"}.get(step[0], "A")


def part(engine, stages):
    return [s for s in STEPS[engine] if stage(s) in stages]


def last_experts(engine):
    up = [[("UP", e, c) for c in range(HC)] for e in range(NE)]
    steps = [("HN",), ("HS",), ("LG",)] + up[0]
    for e in range(NE):
        steps += (up[e + 1] if e + 1 < NE else []) + [("DN", e), ("DN", e, 0), ("DN", e, 1)]
    return [s for s in steps + [("ST",)] if s in STEPS[engine]]


def bank_uses():
    uses, n = {}, 0
    for s in STEPS["pe"]:
        count = {"LD": 2, "QK": 1, "V": 2, "QV": 3, "HN": 1, "LG": 1, "UP": 1}.get(s[0], 0)
        for part_of in range(count):
            uses[(s, part_of)] = f"proj{n % 2}"
            n += 1
        if s[0] in ("W", "XN", "ON"):
            uses[(s, 0)] = "work"
        if s[0] in ("PT", "PV"):
            for half in range(2 if s[0] == "PT" or s[1] == 0 else 1):
                uses[(s, half)] = f"turn{half}"
    assert n % 2 == 0
    return uses


BANK_OF = bank_uses()


def build(nc, x, ctx, m0, m1, m2, wq, wk, wv, wo, gamma, beta, norms, l1w, gw, w1, w2, cos, sin, ident,
          headmask, countdown, out):
    groups = x.shape[0] // G
    xg = x.rearrange("(g t p) d -> g p t d", t=TILES, p=P)
    cg = ctx.rearrange("(g t p) d -> g p t d", t=TILES, p=P)
    og = out.rearrange("(g t p) d -> g p t d", t=TILES, p=P)
    m0g = m0.rearrange("(g t b) k -> g b t k", t=TILES, b=2)
    m1g = m1.rearrange("(g t p) k -> g p t k", t=TILES, p=P)
    m2g = m2.rearrange("(g t p) k -> g p t k", t=TILES, p=P)

    with ExitStack() as stack:
        def sb(name, shape, dt=F32):
            return stack.enter_context(nc.sbuf_tensor(name, shape, dt))

        def sem(name):
            return stack.enter_context(nc.semaphore(name))

        wq_s, wk_s = sb("wq_s", [P, NC0, P]), sb("wk_s", [P, NC0, P])
        wv_s, wo_s = sb("wv_s", [P, H * D0]), sb("wo_s", [P, NC0, P])
        l1w_s = sb("l1w_s", [P, 8, P])
        gw_s = sb("gw_s", [P, E])
        w1_s, w2_s = sb("w1_s", [P, (NE - SPLIT) * HC, P]), sb("w2_s", [P, NE * HC, P])
        w1_hi, w1_lo = sb("w1_hi", [P, SPLIT * HC, P], F32R), sb("w1_lo", [P, SPLIT * HC, P], F32R)
        gamma_s, beta_s = sb("gamma_s", [P, P]), sb("beta_s", [P, P])
        norms_s = sb("norms_s", [P, 3])
        cos_s, sin_s = sb("cos_s", [P, S]), sb("sin_s", [P, S])
        ident_s, ident_b = sb("ident_s", [P, P]), sb("ident_b", [P, P], BF16)
        headmask_s = sb("headmask_s", [P, H // 2])
        countdown_s = sb("countdown_s", [P, E])
        halves = sb("halves", [P, 1])
        x_s, c_s = sb("x_s", [P, TILES, P]), sb("c_s", [P, TILES, P])
        residual = sb("residual", [P, TILES, P])
        m0_s = sb("m0_s", [P, TILES, S], U8)
        m1_s, m2_s = sb("m1_s", [P, TILES, S], I32), sb("m2_s", [P, TILES, S], I32)
        bias = sb("bias", [P, 3, TILES, S], BF16)
        xT, cT, cT1 = sb("xT", [P, G]), sb("cT", [P, G]), sb("cT1", [P, G])
        qk = sb("qk", [P, 2 * NC0, G])
        part_s, part_m = sb("part_s", [P, 2, G]), sb("part_m", [P, 2, G])
        v0 = sb("v0", [P, 2, 2, NC0, 2, D0])
        prob = sb("prob", [P, 2, H * S])
        probT = sb("probT", [P, NC0, P])
        attT = sb("attT", [P, NC0, P])
        rowmax, rowsum, rowinv = sb("rowmax", [P, H]), sb("rowsum", [P, H]), sb("rowinv", [P, H])
        nT = sb("nT", [P, G])
        q1 = sb("q1", [P, G])
        k1 = sb("k1", [P, B, H // 2, S])
        staged = k1[:].rearrange("p b h s -> p (b h s)")[:, 0:SPLIT * HC * P].rearrange("p (c d) -> p c d", d=P)
        v1 = sb("v1", [P, TILES, 2, NC0, 2, D1 + 1])
        inv1 = sb("inv1", [P, H])
        o1, o1T = sb("o1", [P, P]), sb("o1T", [P, P])
        h = sb("h", [P, TILES, P])
        xn = sb("xn", [P, 2, P])
        square, total = sb("square", [P, P]), sb("total", [P, 1])
        var0, rstd0 = sb("var0", [P, TILES]), sb("rstd0", [P, TILES])
        var1, rstd1 = sb("var1", [P, 3, TILES]), sb("rstd1", [P, 3, TILES])
        mean0 = sb("mean0", [P, 1])
        hn3T = sb("hn3T", [P, G])
        hn3T_hi, hn3T_lo = sb("hn3T_hi", [P, G], F32R), sb("hn3T_lo", [P, G], F32R)
        hid = sb("hid", [P, HC, G])
        acc = sb("acc", [P, TILES, P])
        weighted = sb("weighted", [P, TILES, P])
        hn3 = weighted
        lg = sb("lg", [P, TILES, E])
        eq, key = sb("eq", [P, TILES, E]), sb("key", [P, TILES, E])
        first, second, lg2, gates = (sb(n, [P, TILES, E]) for n in ("first", "second", "lg2", "gates"))
        top1, top2, keymax, gap, e2, den, g1, g2 = (
            sb(n, [P, TILES]) for n in ("top1", "top2", "keymax", "gap", "e2", "den", "g1", "g2"))

        banks = stack.enter_context(nc.psum_tensor("banks", [P, 4, 512], F32))
        proj, score = banks[:, 0:2], banks[:, 2:4]
        turn = stack.enter_context(nc.psum_tensor("turn", [P, 2, 512], F32))
        down = stack.enter_context(nc.psum_tensor("down", [P, 512], F32))
        work = stack.enter_context(nc.psum_tensor("work", [P, 512], F32))

        def pj(step, n):
            return proj[:, int(BANK_OF[(step, n)][-1]), :]

        def up_bank(step, alone):
            return banks[:, (HC * step[1] + step[2]) % 4] if alone else pj(step, 0)

        def hid_of(e, alone):
            return qk[:, 0:HC] if alone and e % 2 else hid[:]

        per = {}

        def counted(name, n):
            s = sem(name)
            per[name] = (s, n)
            return name

        for name, n in (
            ("pe_xc", 2), ("pe_qk", 2 * NC0), ("pe_v", TILES), ("pe_s", 3 * TILES), ("pe_pt", 6 * TILES),
            ("pe_pv0", 2 * TILES), ("pe_pv1", 2 * TILES), ("pe_on", 2 * TILES), ("pe_w", 3 * TILES),
            ("pe_xn", 2 * TILES), ("pe_qv", 6), ("pe_h3", 1), ("pe_lg", 1), ("pe_up", NE * HC), ("pe_dn", NE),
            ("act_xc", 2), ("act_v", TILES), ("act_exp", 3 * TILES), ("act_pt", 6 * TILES), ("act_ot", 2 * TILES),
            ("act_on", 2 * TILES), ("act_xn", 2 * TILES), ("act_q1", 2), ("act_v1", 2), ("act_h3", 1),
            ("act_e2", 1), ("act_tanh", NE * HC), ("act_cT1", 1), ("act_k1", 2),
            ("dve_bias", 3), ("dve_split", 1), ("dve_cos", 2 * NC0), ("dve_sin", 2 * NC0), ("dve_sub", 3 * TILES),
            ("dve_inv", TILES), ("dve_k1", 2), ("dve_on", 2 * TILES), ("dve_w", 3 * TILES),
            ("dve_var0", TILES), ("dve_var1", 3 * TILES), ("dve_ln", TILES), ("dve_xn", 2 * TILES), ("dve_hn3", 1),
            ("dve_lg", 1), ("dve_hid", NE * HC), ("dve_gap", 1), ("dve_gates", 1), ("dve_wt", NE),
            ("pool_qk", 2 * NC0), ("pool_norm", TILES), ("pool_rstd0", TILES), ("pool_rstd1", 3 * TILES),
            ("pool_acc", NE),
        ):
            counted(name, n)
        s_w0, s_wv, s_w1, s_w2, s_l1 = sem("load_wqk"), sem("load_wv"), sem("load_w1"), sem("load_w2"), sem("load_l1")
        s_tab = sem("load_tables")
        s_x, s_c, s_m, s_res = sem("load_x"), sem("load_ctx"), sem("load_masks"), sem("load_residual")
        s_move = [sem("partners_moved0"), sem("partners_moved1")]
        s_out = sem("stored")
        s_init, s_idb = sem("buffers_initialised"), sem("identity_bf16")
        s_split = sem("w1_split")
        s_chainA, s_chainB = sem("vector_chain_a"), sem("vector_chain_b")

        def after(eng, name, it, n):
            s, k = per[name]
            eng.wait_ge(s, it * k + (n + 1))

        def done(ins, name):
            ins.then_inc(per[name][0], 1)

        def is_zero(it):
            return isinstance(it, int) and it == 0

        def readers(step, n):
            kind = step[0]
            if kind == "LD":
                return [("act_xc", n)]
            if kind == "QK":
                return [("dve_sin", step[1])]
            if kind == "V":
                return [("act_v", step[1])]
            if kind == "QV":
                g = step[1] - 1
                return ([("act_q1", g)], [("act_k1", g)], [("act_v1", g)])[n]
            if kind == "HN":
                return [("act_h3", 0)]
            if kind == "LG":
                return [("dve_lg", 0)]
            if kind == "UP":
                return [("dve_hid", HC * step[1] + step[2])]
            if kind == "W":
                return [("dve_w", TILES * step[1] + step[2])]
            if kind == "XN":
                return [("act_xn", TILES * (step[1] - 1) + step[2])]
            if kind == "ON":
                return [("act_on", TILES * (step[1] - 1) + step[2])]
            if kind == "PT":
                return [("act_pt", 2 * (TILES * step[1] + step[2]) + n)]
            if kind == "PV":
                return [("act_ot", 2 * step[2] + n) if step[1] == 0 else ("dve_on", TILES * (step[1] - 1) + step[2])]

        def bank_free(pe, steps, step, n, of):
            bank = BANK_OF[(step, n)]
            uses = [(s, m) for s in steps for m in range(HC) if BANK_OF.get((s, m)) == bank]
            at = uses.index((step, n))
            if at:
                s, m = uses[at - 1]
                for name, k in readers(s, m):
                    after(pe, name, of[stage(s)], k)
                return
            for st in "ABC":
                mine = [(s, m) for s in STEPS["pe"] for m in range(HC) if BANK_OF.get((s, m)) == bank and stage(s) == st]
                if mine and not is_zero(of[st]):
                    for name, _ in readers(*mine[-1]):
                        sm, count = per[name]
                        pe.wait_ge(sm, of[st] * count)

        block = stack.enter_context(nc.Block())

        @block.sync
        def _(sp):
            sp.dma_start(cos_s[:], cos).then_inc(s_tab, 16)
            sp.dma_start(sin_s[:], sin).then_inc(s_tab, 16)
            sp.dma_start(ident_s[:], ident).then_inc(s_tab, 16)
            sp.dma_start(headmask_s[:], headmask).then_inc(s_tab, 16)
            sp.dma_start(countdown_s[:], countdown).then_inc(s_tab, 16)
            sp.dma_start(gamma_s[:], gamma.partition_broadcast(P)).then_inc(s_tab, 16)
            sp.dma_start(beta_s[:], beta.partition_broadcast(P)).then_inc(s_tab, 16)
            sp.dma_start(norms_s[:], norms).then_inc(s_tab, 16)

            def iteration(ia, first):
                def released(name, n):
                    if not first:
                        after(sp, name, ia - 1, n)

                released("pe_xc", 1)
                sp.dma_start(x_s[:], xg[ia]).then_inc(s_x, 16)
                sp.dma_start(c_s[:], cg[ia]).then_inc(s_c, 16)
                released("dve_w", TILES - 1)
                sp.dma_start(residual[:], xg[ia]).then_inc(s_res, 16)
                for b in range(2):
                    sp.dma_start(m0_s[b * S:(b + 1) * S], m0g[ia, b].partition_broadcast(S)).then_inc(s_m, 16)
                sp.dma_start(m1_s[:], m1g[ia]).then_inc(s_m, 16)
                sp.dma_start(m2_s[:], m2g[ia]).then_inc(s_m, 16)
                if first:
                    sp.dma_start(wq_s[:], wq).then_inc(s_w0, 16)
                    sp.dma_start(wk_s[:], wk).then_inc(s_w0, 16)
                    sp.dma_start(wv_s[:], wv).then_inc(s_wv, 16)
                    sp.dma_start(wo_s[:], wo).then_inc(s_wv, 16)
                    sp.dma_start(l1w_s[:], l1w).then_inc(s_l1, 16)
                    sp.dma_start(gw_s[:], gw).then_inc(s_l1, 16)
                    sp.dma_start(staged, w1[:, 0:SPLIT * HC]).then_inc(s_w1, 16)
                    sp.dma_start(w1_s[:], w1[:, SPLIT * HC:]).then_inc(s_w1, 16)
                    sp.dma_start(w2_s[:], w2).then_inc(s_w2, 16)
                for n in range(2 * NC0):
                    after(sp, "dve_sin", ia, n)
                    r = n % 2
                    for quad in range(4):
                        to = quad ^ 1
                        sp.dma_start(part_m[32 * to:32 * to + 32, r], part_s[32 * quad:32 * quad + 32, r])\
                          .then_inc(s_move[r], 16)

            iteration(0, True)
            iteration(1, False)
            with sp.Fori(2, groups) as i:
                iteration(i, False)

        @block.gpsimd
        def _(pool):
            nc.gpsimd.memset(halves[:], -0.5).then_inc(s_init, 1)
            nc.gpsimd.memset(v0[:], 0.0).then_inc(s_init, 1)
            nc.gpsimd.memset(v1[:], 0.0).then_inc(s_init, 1)
            pool.wait_ge(s_init, 3)
            for cc in range(2):
                nc.gpsimd.memset(v1[cc * S:(cc + 1) * S, :, :, :, cc, D1:D1 + 1], 1.0).then_inc(s_init, 1)
            pool.wait_ge(s_init, 5)

            def iteration(ia, ib, ic, steps, alone=False):
                for step in steps:
                    kind = step[0]
                    if kind == "QK":
                        n = step[1]
                        pool.wait_ge(s_move[n % 2], 64 * (n // 2 + 1) + ic * (64 * NC0))
                        done(nc.gpsimd.tensor_tensor(qk[:, n], qk[:, n], part_m[:, n % 2], ALU.add), "pool_qk")
                    elif kind == "PT" and step[1] == 0:
                        t = step[2]
                        after(pool, "dve_inv", ia, t)
                        pr = prob[:, t % 2].rearrange("p (h k) -> p h k", h=H)
                        done(nc.gpsimd.tensor_tensor(pr, pr, rowinv[:].unsqueeze(2).to_broadcast([P, H, S]), ALU.mult),
                             "pool_norm")
                    elif kind == "W":
                        a, t = step[1:]
                        if a == 0:
                            after(pool, "dve_var0", ia, t)
                            done(nc.gpsimd.tensor_tensor(rstd0[:, t:t + 1], var0[:, t:t + 1], halves[:], ALU.pow), "pool_rstd0")
                        else:
                            after(pool, "dve_var1", ia, TILES * a + t)
                            done(nc.gpsimd.tensor_tensor(rstd1[:, a, t:t + 1], var1[:, a, t:t + 1], halves[:], ALU.pow),
                                 "pool_rstd1")
                    elif kind == "LN":
                        t = step[1]
                        after(pool, "dve_var1", ia, t)
                        done(nc.gpsimd.tensor_tensor(rstd1[:, 0, t:t + 1], var1[:, 0, t:t + 1], halves[:], ALU.pow),
                             "pool_rstd1")
                    elif kind == "DN":
                        e = step[1]
                        after(pool, "dve_wt", ib, e)
                        if e == 0:
                            if not is_zero(ib):
                                pool.wait_ge(s_out, ib * 16)
                        else:
                            after(pool, "pool_acc", ib, e - 1)
                        done(nc.gpsimd.tensor_tensor(acc[:], acc[:] if e else h[:], weighted[:], ALU.add), "pool_acc")

            iteration(0, 0, 0, part("pool", "C"))
            pool.wait_ge(s_w1, 32)
            nc.gpsimd.tensor_copy(w1_hi[:], staged).then_inc(s_split, 1)
            pool.wait_ge(s_split, 1)
            nc.gpsimd.tensor_tensor(w1_lo[:], staged, w1_hi[:].bitcast(F32), ALU.subtract).then_inc(s_split, 1)
            iteration(0, 0, 1, part("pool", "AC"))
            iteration(1, 0, 2, part("pool", "ABC"))
            with pool.Fori(2, groups - 1) as i:
                iteration(i, i - 1, i + 1, part("pool", "ABC"))
            iteration(groups - 1, groups - 2, groups, part("pool", "AB"))
            iteration(groups, groups - 1, groups, last_experts("pool"), alone=True)

        @block.scalar
        def _(act):
            def iteration(ia, ib, ic, steps, alone=False):
                for step in steps:
                    kind = step[0]
                    if kind == "LD":
                        if not is_zero(ic):
                            after(act, "pe_v", ic - 1, TILES - 1)
                        for n, dst in enumerate((xT, cT)):
                            after(act, "pe_xc", ic, n)
                            done(nc.scalar.copy(dst[:], pj(step, n)), "act_xc")
                    elif kind == "V":
                        t = step[1]
                        after(act, "pe_v", ia, t)
                        if is_zero(ia) and t == 0:
                            act.wait_ge(s_init, 5)
                        if t >= 2:
                            after(act, "pe_pv0", ia, 2 * (t - 2) + 1)
                        elif not is_zero(ia):
                            after(act, "pe_pv0", ia - 1, 2 * (t + 2) + 1)
                        for b in range(2):
                            for cc in range(2):
                                src = proj[b * S:(b + 1) * S].rearrange("p n (j c d) -> p (n j) c d", c=2, d=D0)[:, :, cc]
                                ins = nc.scalar.copy(v0[cc * S:(cc + 1) * S, t % 2, b, :, cc], src)
                        done(ins, "act_v")
                        if t == 0:
                            if not is_zero(ia):
                                after(act, "pe_qv", ia - 1, 5)
                            after(act, "act_xc", ia, 1)
                            done(nc.scalar.copy(cT1[:], cT[:]), "act_cT1")
                    elif kind == "S":
                        a, t = step[1:]
                        after(act, "dve_sub", ia, TILES * a + t)
                        done(nc.scalar.activation(prob[:, t % 2], prob[:, t % 2], ACT.Exp,
                                                  scale=float((D1 if a else D0) ** -0.5)), "act_exp")
                    elif kind == "PT":
                        a, t = step[1:]
                        for half in range(2):
                            after(act, "pe_pt", ia, 2 * (TILES * a + t) + half)
                            if a > 1 or a == 1 and t:
                                after(act, "pe_pv1", ia, TILES * (a - 1) + t - 1)
                            elif a or t:
                                after(act, "pe_pv0", ia, 2 * (TILES * a + t - 1) + half)
                            elif not is_zero(ia):
                                after(act, "pe_pv1", ia - 1, 2 * TILES - 1)
                            done(nc.scalar.copy(probT[:, 4 * half:4 * half + 4], turn[:, half, :]), "act_pt")
                    elif kind == "PV" and step[1] == 0:
                        t = step[2]
                        for half in range(2):
                            after(act, "pe_pv0", ia, 2 * t + half)
                            if t:
                                after(act, "pe_w", ia, t - 1)
                            elif not is_zero(ia):
                                after(act, "pe_w", ia - 1, TILES - 1)
                            done(nc.scalar.copy(attT[:, 4 * half:4 * half + 4], turn[:, half, :]), "act_ot")
                    elif kind == "XN":
                        a, t = step[1:]
                        after(act, "pe_xn", ia, TILES * (a - 1) + t)
                        if is_zero(ia) and a == 1 and t == 0:
                            act.wait_ge(s_tab, 8 * 16)
                        done(nc.scalar.mul(nT[:, t * P:(t + 1) * P], work[:, 0:P], norms_s[:, a - 1:a]), "act_xn")
                    elif kind == "QV":
                        a = step[1]
                        after(act, "pe_qv", ia, 3 * (a - 1))
                        done(nc.scalar.copy(q1[:], pj(step, 0)), "act_q1")
                        after(act, "pe_qv", ia, 3 * (a - 1) + 1)
                        if is_zero(ia) and a == 1:
                            act.wait_ge(s_split, 2)
                        done(nc.scalar.copy(k1[:, :, H // 2 - 1], pj(step, 1).rearrange("p (b s) -> p b s", b=B)), "act_k1")
                        after(act, "pe_qv", ia, 3 * (a - 1) + 2)
                        src = pj(step, 2).rearrange("p (t j c d) -> p t j c d", t=TILES, c=2, d=D1)
                        for b in range(2):
                            for cc in range(2):
                                ins = nc.scalar.copy(v1[cc * S:(cc + 1) * S, :, b, :, cc, 0:D1],
                                                     src[b * S:(b + 1) * S, :, :, cc])
                        done(ins, "act_v1")
                    elif kind == "ON":
                        a, t = step[1:]
                        after(act, "pe_on", ia, TILES * (a - 1) + t)
                        if t or a > 1:
                            after(act, "pe_w", ia, TILES * a + t - 1)
                        elif not is_zero(ia):
                            after(act, "pe_w", ia - 1, 3 * TILES - 1)
                        done(nc.scalar.copy(o1T[:], work[:, 0:P]), "act_on")
                    elif kind == "HN":
                        after(act, "pe_h3", ib, 0)
                        done(nc.scalar.mul(hn3T[:], pj(step, 0), norms_s[:, 2:3]), "act_h3")
                    elif kind == "LG":
                        after(act, "dve_gap", ib, 0)
                        done(nc.scalar.activation(e2[:], gap[:], ACT.Exp), "act_e2")
                    elif kind == "UP":
                        e, c = step[1:]
                        after(act, "pe_up", ib, HC * e + c)
                        if e >= 2 or e and not alone:
                            after(act, "pe_dn", ib, e - (2 if alone else 1))
                        elif not is_zero(ib):
                            after(act, "pe_dn", ib - 1, NE - 1)
                        done(nc.scalar.activation(hid_of(e, alone)[:, c], up_bank(step, alone), ACT.Tanh, scale=0.5), "act_tanh")
                    elif kind == "ST":
                        after(act, "pool_acc", ib, NE - 1)
                        act.dma_start(og[ib], acc[:]).then_inc(s_out, 16)

            iteration(0, 0, 0, part("act", "C"))
            iteration(0, 0, 1, part("act", "AC"))
            iteration(1, 0, 2, part("act", "ABC"))
            with act.Fori(2, groups - 1) as i:
                iteration(i, i - 1, i + 1, part("act", "ABC"))
            iteration(groups - 1, groups - 2, groups, part("act", "AB"))
            iteration(groups, groups - 1, groups, last_experts("act"), alone=True)
            act.wait_ge(s_out, groups * 16)

        LINKS_A, LINKS_B = 58, 19

        @block.vector
        def _(dve):
            dve.wait_ge(s_tab, 8 * 16)
            nc.vector.tensor_copy(ident_b[:], ident_s[:]).then_inc(s_idb, 1)

            def iteration(ia, ib, ic, steps, alone=False):
                links = {"A": 0, "B": 0}

                def link(ins, which="A"):
                    s, it, k = (s_chainA, ia, LINKS_A) if which == "A" else (s_chainB, ib, LINKS_B)
                    links[which] += 1
                    ins.then_inc(s, 1)
                    dve.wait_ge(s, it * k + links[which])

                def mean_square(src, dst, a, t):
                    link(nc.vector.tensor_tensor_reduce(out=square[:], in0=src, in1=src, scale=1.0, scalar=0.0,
                                                        op0=ALU.mult, op1=ALU.add, accum_out=total[:]))
                    done(nc.vector.tensor_scalar(dst, total[:], 1.0 / P, 1e-5, ALU.mult, ALU.add), "dve_var1")

                for step in steps:
                    kind = step[0]
                    if kind == "MB":
                        dve.wait_ge(s_m, 64 * (ic + 1))
                        if not is_zero(ic):
                            after(dve, "pe_s", ic - 1, 3 * TILES - 1)
                        for n, m in enumerate((m0_s, m1_s, m2_s)):
                            done(nc.vector.tensor_scalar(bias[:, n], m[:], 0.0, MASKED, ALU.is_equal, ALU.mult), "dve_bias")
                    elif kind == "QK":
                        n = step[1]
                        after(dve, "pe_qk", ic, n)
                        if not is_zero(ic):
                            after(dve, "pe_s", ic - 1, TILES - 1)
                        src = pj(step, 0).rearrange("p (b s) -> p b s", b=B)
                        tab = [tb[:].unsqueeze(1).to_broadcast([P, B, S]) for tb in (cos_s, sin_s)]
                        done(nc.vector.tensor_tensor(qk[:, n].rearrange("p (b s) -> p b s", b=B), src, tab[0], ALU.mult),
                             "dve_cos")
                        if n >= 2:
                            after(dve, "pool_qk", ic, n - 2)
                        elif not is_zero(ic):
                            after(dve, "pool_qk", ic - 1, n + 2 * NC0 - 2)
                        done(nc.vector.tensor_tensor(part_s[:, n % 2].rearrange("p (b s) -> p b s", b=B),
                                                     src, tab[1], ALU.mult), "dve_sin")
                    elif kind == "S":
                        a, t = step[1:]
                        after(dve, "pe_s", ia, TILES * a + t)
                        sc = score[:].rearrange("p n (h k) -> p (n h) k", k=S)
                        pr = prob[:, t % 2].rearrange("p (h k) -> p h k", h=H)
                        link(nc.vector.tensor_reduce(rowmax[:], sc, AX.X, ALU.max))
                        if a or t >= 2:
                            after(dve, "pe_pt", ia, 2 * (TILES * a + t - 2) + 1)
                        elif not is_zero(ia):
                            after(dve, "pe_pt", ia - 1, 2 * (3 * TILES + t - 2) + 1)
                        done(nc.vector.tensor_tensor(pr, sc, rowmax[:].unsqueeze(2).to_broadcast([P, H, S]), ALU.subtract),
                             "dve_sub")
                    elif kind == "SM":
                        t = step[1]
                        after(dve, "act_exp", ia, t)
                        if t:
                            after(dve, "dve_inv", ia, t - 1)
                        elif not is_zero(ia):
                            after(dve, "dve_inv", ia - 1, TILES - 1)
                        link(nc.vector.tensor_reduce(rowsum[:], prob[:, t % 2].rearrange("p (h k) -> p h k", h=H), AX.X, ALU.add))
                        if t:
                            after(dve, "pool_norm", ia, t - 1)
                        elif not is_zero(ia):
                            after(dve, "pool_norm", ia - 1, TILES - 1)
                        done(nc.vector.reciprocal(rowinv[:], rowsum[:]), "dve_inv")
                    elif kind == "W":
                        a, t = step[1:]
                        after(dve, "pe_w", ia, TILES * a + t)
                        ht = h[:, t]
                        if a == 0:
                            if t == 0:
                                dve.wait_ge(s_res, 16 * (ia + 1))
                            if t == 0 and not is_zero(ia):
                                after(dve, "pool_acc", ib, 0)
                            done(nc.vector.tensor_tensor(ht, residual[:, t], work[:, 0:P], ALU.add), "dve_w")
                            after(dve, "dve_w", ia, t)
                            link(nc.vector.tensor_reduce(total[:], ht, AX.X, ALU.add))
                            link(nc.vector.tensor_scalar(mean0[:], total[:], 1.0 / P, None, ALU.mult))
                            link(nc.vector.tensor_scalar(ht, ht, mean0[:], None, ALU.subtract))
                            link(nc.vector.tensor_tensor_reduce(out=square[:], in0=ht, in1=ht, scale=1.0, scalar=0.0,
                                                                op0=ALU.mult, op1=ALU.add, accum_out=total[:]))
                            done(nc.vector.tensor_scalar(var0[:, t:t + 1], total[:], 1.0 / P, 1e-3, ALU.mult, ALU.add),
                                 "dve_var0")
                        else:
                            done(nc.vector.tensor_tensor(ht, ht, work[:, 0:P], ALU.add), "dve_w")
                            after(dve, "dve_w", ia, TILES * a + t)
                            mean_square(ht, var1[:, a, t:t + 1], a, t)
                    elif kind == "LN":
                        t = step[1]
                        ht = h[:, t]
                        after(dve, "pool_rstd0", ia, t)
                        link(nc.vector.scalar_tensor_tensor(out=ht, in0=ht, scalar=rstd0[:, t:t + 1], in1=gamma_s[:],
                                                            op0=ALU.mult, op1=ALU.mult))
                        done(nc.vector.tensor_tensor(ht, ht, beta_s[:], ALU.add), "dve_ln")
                        after(dve, "dve_ln", ia, t)
                        mean_square(ht, var1[:, 0, t:t + 1], 0, t)
                    elif kind == "RN":
                        a, t = step[1:]
                        after(dve, "pool_rstd1", ia, TILES * (a - 1) + t)
                        if t >= 2:
                            after(dve, "pe_xn", ia, TILES * (a - 1) + t - 2)
                        done(nc.vector.tensor_scalar(xn[:, t % 2], h[:, t], rstd1[:, a - 1, t:t + 1], None, ALU.mult),
                             "dve_xn")
                    elif kind == "QV":
                        a = step[1]
                        after(dve, "act_k1", ia, a - 1)
                        kp = k1[:, :, H // 2 - 1]
                        for hh in range(H // 2):
                            if hh == H // 2 - 1:
                                link(ins)
                            ins = nc.vector.tensor_scalar(k1[:, :, hh], kp, headmask_s[:, hh:hh + 1], None, ALU.mult)
                        done(ins, "dve_k1")
                    elif kind == "PV" and step[1]:
                        a, t = step[1:]
                        after(dve, "pe_pv1", ia, TILES * (a - 1) + t)
                        o = turn[:, 0, 0:H * (D1 + 1)].rearrange("p (h d) -> p h d", h=H)
                        link(nc.vector.reciprocal(inv1[:], o[:, :, D1]))
                        if t or a > 1:
                            after(dve, "pe_on", ia, TILES * (a - 1) + t - 1)
                        elif not is_zero(ia):
                            after(dve, "pe_on", ia - 1, 2 * TILES - 1)
                        done(nc.vector.tensor_tensor(o1[:].rearrange("p (h d) -> p h d", h=H), o[:, :, 0:D1],
                                                     inv1[:].unsqueeze(2).to_broadcast([P, H, D1]), ALU.mult), "dve_on")
                    elif kind == "HN":
                        after(dve, "pool_rstd1", ib, 3 * TILES - 1)
                        if not is_zero(ib):
                            after(dve, "pool_acc", ib - 1, NE - 1)
                        for t in range(TILES):
                            ins = nc.vector.tensor_scalar(hn3[:, t], h[:, t], rstd1[:, 2, t:t + 1], None, ALU.mult)
                        done(ins, "dve_hn3")
                    elif kind == "HS":
                        after(dve, "act_h3", ib, 0)
                        link(nc.vector.tensor_copy(hn3T_hi[:], hn3T[:]), "B")
                        done(nc.vector.tensor_tensor(hn3T_lo[:], hn3T[:], hn3T_hi[:].bitcast(F32), ALU.subtract), "dve_split")
                    elif kind == "LG":
                        def wide(v):
                            return v[:].unsqueeze(2).to_broadcast([P, TILES, E])
                        cd = countdown_s[:].unsqueeze(1).to_broadcast([P, TILES, E])
                        after(dve, "pe_lg", ib, 0)
                        done(nc.vector.tensor_copy(lg[:], pj(step, 0)[:, 0:TILES * E].rearrange("p (t e) -> p t e", e=E)), "dve_lg")
                        after(dve, "dve_lg", ib, 0)
                        for src, top, pick in ((lg, top1, first_of["first"]), (lg2, top2, first_of["second"])):
                            link(nc.vector.tensor_reduce(top[:], src[:], AX.X, ALU.max), "B")
                            link(nc.vector.tensor_tensor(eq[:], src[:], wide(top), ALU.is_equal), "B")
                            link(nc.vector.tensor_tensor(key[:], eq[:], cd, ALU.mult), "B")
                            link(nc.vector.tensor_reduce(keymax[:], key[:], AX.X, ALU.max), "B")
                            link(nc.vector.tensor_tensor(pick[:], key[:], wide(keymax), ALU.is_equal), "B")
                            if src is lg:
                                link(nc.vector.tensor_scalar(lg2[:], pick[:], -BIG, None, ALU.mult), "B")
                                link(nc.vector.tensor_tensor(lg2[:], lg2[:], lg[:], ALU.add), "B")
                        done(nc.vector.tensor_tensor(gap[:], top2[:], top1[:], ALU.subtract), "dve_gap")
                        after(dve, "act_e2", ib, 0)
                        link(nc.vector.tensor_scalar_add(den[:], e2[:], 1.0), "B")
                        link(nc.vector.reciprocal(g1[:], den[:]), "B")
                        link(nc.vector.tensor_scalar(g1[:], g1[:], 0.5, None, ALU.mult), "B")
                        link(nc.vector.tensor_tensor(g2[:], e2[:], g1[:], ALU.mult), "B")
                        link(nc.vector.tensor_tensor(gates[:], first_of["first"][:], wide(g1), ALU.mult), "B")
                        link(nc.vector.tensor_tensor(key[:], first_of["second"][:], wide(g2), ALU.mult), "B")
                        done(nc.vector.tensor_tensor(gates[:], gates[:], key[:], ALU.add), "dve_gates")
                    elif kind == "UP":
                        e, c = step[1:]
                        after(dve, "act_tanh", ib, HC * e + c)
                        buf = hid_of(e, alone)[:, c]
                        done(nc.vector.scalar_tensor_tensor(out=buf, in0=buf, scalar=1.0, in1=up_bank(step, alone),
                                                            op0=ALU.add, op1=ALU.mult), "dve_hid")
                    elif kind == "DN":
                        e = step[1]
                        after(dve, "pe_dn", ib, e)
                        if e:
                            after(dve, "pool_acc", ib, e - 1)
                        src = down[:].rearrange("p (t d) -> p t d", t=TILES)
                        if e == 0:
                            done(nc.vector.tensor_scalar(weighted[:], src, 0.5, None, ALU.mult), "dve_wt")
                        else:
                            if e == 1:
                                after(dve, "dve_gates", ib, 0)
                            done(nc.vector.tensor_tensor(weighted[:], src,
                                                         gates[:, :, e - 1:e].to_broadcast([P, TILES, P]), ALU.mult), "dve_wt")
                assert links["A"] in (0, LINKS_A) and links["B"] in (0, LINKS_B), links

            first_of = {"first": first, "second": second}
            iteration(0, 0, 0, part("dve", "C"))
            iteration(0, 0, 1, part("dve", "AC"))
            iteration(1, 0, 2, part("dve", "ABC"))
            with dve.Fori(2, groups - 1) as i:
                iteration(i, i - 1, i + 1, part("dve", "ABC"))
            iteration(groups - 1, groups - 2, groups, part("dve", "AB"))
            iteration(groups, groups - 1, groups, last_experts("dve"), alone=True)

        @block.tensor
        def _(pe):
            def iteration(ia, ib, ic, steps, alone=False):
                for step in steps:
                    kind = step[0]

                    def free(n=0):
                        bank_free(pe, steps, step, n, {"A": ia, "B": ib, "C": ic})

                    if kind == "LD":
                        for n, (src, s) in enumerate(((x_s, s_x), (c_s, s_c))):
                            if is_zero(ic):
                                pe.wait_ge(s_tab, 8 * 16)
                            pe.wait_ge(s, 16 * (ic + 1))
                            free(n)
                            for t in range(TILES):
                                ins = nc.tensor.transpose(pj(step, n)[:, t * P:(t + 1) * P], src[:, t], ident_s[:])
                            done(ins, "pe_xc")
                    elif kind == "QK":
                        n = step[1]
                        free()
                        if n == 0:
                            after(pe, "act_xc", ic, 1)
                            if is_zero(ic):
                                pe.wait_ge(s_w0, 32)
                        w, src = (wq_s, xT) if n < NC0 else (wk_s, cT)
                        done(nc.tensor.matmul(pj(step, 0), w[:, n % NC0], src[:], start=True, stop=True), "pe_qk")
                    elif kind == "V":
                        t = step[1]
                        if is_zero(ia) and t == 0:
                            pe.wait_ge(s_wv, 32)
                        for n in range(2):
                            free(n)
                            half = int(BANK_OF[(step, n)][-1])
                            ins = nc.tensor.matmul(pj(step, n), cT[:, t * P:(t + 1) * P],
                                                   wv_s[:, half * 512:(half + 1) * 512], start=True, stop=True)
                        done(ins, "pe_v")
                    elif kind == "S":
                        a, t = step[1:]
                        if a or t:
                            after(pe, "dve_sub", ia, TILES * a + t - 1)
                        elif not is_zero(ia):
                            after(pe, "dve_sub", ia - 1, 3 * TILES - 1)
                        if t == 0:
                            if a == 0:
                                after(pe, "dve_bias", ia, 2)
                                after(pe, "pool_qk", ia, 2 * NC0 - 1)
                                if is_zero(ia):
                                    pe.wait_ge(s_idb, 1)
                            else:
                                after(pe, "act_q1", ia, a - 1)
                                after(pe, "dve_k1", ia, a - 1)
                        for hp in range(2):
                            nc.tensor.matmul(score[:, hp].rearrange("p (h k) -> p h k", k=S), ident_b[:],
                                             bias[:, a, t].unsqueeze(1).to_broadcast([P, H // 2, S]), start=True, stop=True)
                        ts = t * P
                        if a == 0:
                            for c in range(NC0):
                                for hp in range(2):
                                    for b in range(2):
                                        rows = slice(hp * D0, hp * D0 + D0)
                                        tok = slice(ts + b * S, ts + b * S + S)
                                        ins = nc.tensor.matmul(score[b * S:(b + 1) * S, hp, c * S:(c + 1) * S],
                                                               qk[rows, c, tok], qk[rows, NC0 + c, tok],
                                                               start=False, stop=True, skip_group_check=True)
                        else:
                            for b in range(2):
                                for hp in range(2):
                                    rows = slice(hp * 64, hp * 64 + 64)
                                    ins = nc.tensor.matmul(score[b * S:(b + 1) * S, hp], q1[rows, ts + b * S:ts + b * S + S],
                                                           k1[rows, 2 * t + b].rearrange("p h k -> p (h k)"),
                                                           start=False, stop=True, skip_group_check=True)
                        done(ins, "pe_s")
                    elif kind == "PT":
                        a, t = step[1:]
                        if a == 0:
                            after(pe, "pool_norm", ia, t)
                        else:
                            after(pe, "act_exp", ia, TILES * a + t)
                        for half in range(2):
                            free(half)
                            for j in range(4):
                                jj = 4 * half + j
                                ins = nc.tensor.transpose(turn[:, half, j * P:(j + 1) * P],
                                                          prob[:, t % 2, jj * P:(jj + 1) * P], ident_s[:])
                            done(ins, "pe_pt")
                    elif kind == "PV":
                        a, t = step[1:]
                        if a == 0:
                            after(pe, "act_v", ia, t)
                        elif t == 0:
                            after(pe, "act_v1", ia, a - 1)
                        if a == 0:
                            for half in range(2):
                                free(half)
                                after(pe, "act_pt", ia, 2 * (TILES * a + t) + half)
                                for j in range(4):
                                    for b in range(2):
                                        jj = 4 * half + j
                                        ins = nc.tensor.matmul(turn[:, half, j * P + b * S:j * P + (b + 1) * S],
                                                               v0[:, t % 2, b, jj].rearrange("p c d -> p (c d)"),
                                                               probT[:, jj, b * S:(b + 1) * S], start=True, stop=True)
                                done(ins, "pe_pv0")
                        else:
                            free(0)
                            after(pe, "act_pt", ia, 2 * (TILES * a + t) + 1)
                            for j in range(NC0):
                                for b in range(2):
                                    w = 2 * (D1 + 1)
                                    ins = nc.tensor.matmul(turn[b * S:(b + 1) * S, 0, j * w:(j + 1) * w],
                                                           probT[:, j, b * S:(b + 1) * S],
                                                           v1[:, t, b, j].rearrange("p c d -> p (c d)"), start=True, stop=True)
                            done(ins, "pe_pv1")
                    elif kind == "W":
                        a, t = step[1:]
                        free()
                        if a == 0:
                            after(pe, "act_ot", ia, 2 * t + 1)
                            for j in range(NC0):
                                ins = nc.tensor.matmul(work[:, 0:P], attT[:, j], wo_s[:, j], start=j == 0, stop=j == NC0 - 1)
                        else:
                            after(pe, "act_on", ia, TILES * (a - 1) + t)
                            ins = nc.tensor.matmul(work[:, 0:P], o1T[:], l1w_s[:, 4 * (a - 1) + 3], start=True, stop=True)
                        done(ins, "pe_w")
                    elif kind == "XN":
                        a, t = step[1:]
                        free()
                        after(pe, "dve_xn", ia, TILES * (a - 1) + t)
                        done(nc.tensor.transpose(work[:, 0:P], xn[:, t % 2], ident_s[:]), "pe_xn")
                    elif kind == "ON":
                        a, t = step[1:]
                        free()
                        after(pe, "dve_on", ia, TILES * (a - 1) + t)
                        done(nc.tensor.transpose(work[:, 0:P], o1[:], ident_s[:]), "pe_on")
                    elif kind == "QV":
                        a = step[1]
                        if is_zero(ia) and a == 1:
                            pe.wait_ge(s_l1, 32)
                        after(pe, "act_xn", ia, TILES * a - 1)
                        src = nT if a == 1 else cT1
                        if a == 2:
                            after(pe, "act_cT1", ia, 0)
                        free(0)
                        done(nc.tensor.matmul(pj(step, 0), l1w_s[:, 4 * (a - 1)], nT[:], start=True, stop=True), "pe_qv")
                        free(1)
                        done(nc.tensor.matmul(pj(step, 1), l1w_s[:, 4 * (a - 1) + 1], src[:], start=True, stop=True), "pe_qv")
                        free(2)
                        for t in range(TILES):
                            ins = nc.tensor.matmul(pj(step, 2)[:, t * P:(t + 1) * P], src[:, t * P:(t + 1) * P],
                                                   l1w_s[:, 4 * (a - 1) + 2], start=True, stop=True)
                        done(ins, "pe_qv")
                    elif kind == "HN":
                        free()
                        after(pe, "dve_hn3", ib, 0)
                        for t in range(TILES):
                            ins = nc.tensor.transpose(pj(step, 0)[:, t * P:(t + 1) * P], hn3[:, t], ident_s[:])
                        done(ins, "pe_h3")
                    elif kind == "LG":
                        free()
                        after(pe, "act_h3", ib, 0)
                        for t in range(TILES):
                            ins = nc.tensor.matmul(pj(step, 0)[:, t * E:(t + 1) * E], hn3T[:, t * P:(t + 1) * P], gw_s[:],
                                                   start=True, stop=True)
                        done(ins, "pe_lg")
                    elif kind == "UP":
                        e, c = step[1:]
                        if e == 0 and c == 0:
                            pe.wait_ge(s_split, 2)
                            after(pe, "dve_split", ib, 0)
                        if not alone:
                            free()
                        elif e:
                            after(pe, "dve_hid", ib, HC * (e - 1) + c)
                        else:
                            after(pe, "dve_lg", ib, 0)
                        z = up_bank(step, alone)
                        if e < SPLIT:
                            nc.tensor.matmul(z, w1_lo[:, HC * e + c], hn3T_hi[:], start=True, stop=False)
                            nc.tensor.matmul(z, w1_hi[:, HC * e + c], hn3T_lo[:], start=False, stop=False)
                            ins = nc.tensor.matmul(z, w1_hi[:, HC * e + c], hn3T_hi[:], start=False, stop=True)
                        else:
                            ins = nc.tensor.matmul(z, w1_s[:, HC * (e - SPLIT) + c], hn3T[:], start=True, stop=True)
                        done(ins, "pe_up")
                    elif kind == "DN":
                        e, half = step[1:]
                        if half:
                            pass
                        elif e == 0:
                            pe.wait_ge(s_w2, 16)
                            if not is_zero(ib):
                                after(pe, "dve_wt", ib - 1, NE - 1)
                        else:
                            after(pe, "dve_wt", ib, e - 1)
                        if not half:
                            after(pe, "dve_hid", ib, HC * e + HC - 1)
                        for t in (2 * half, 2 * half + 1):
                            for c in range(HC):
                                ins = nc.tensor.matmul(down[:, t * P:(t + 1) * P], hid_of(e, alone)[:, c, t * P:(t + 1) * P],
                                                       w2_s[:, HC * e + c], start=c == 0, stop=c == HC - 1)
                        if half:
                            done(ins, "pe_dn")

            iteration(0, 0, 0, part("pe", "C"))
            iteration(0, 0, 1, part("pe", "AC"))
            iteration(1, 0, 2, part("pe", "ABC"))
            with pe.Fori(2, groups - 1) as i:
                iteration(i, i - 1, i + 1, part("pe", "ABC"))
            iteration(groups - 1, groups - 2, groups, part("pe", "AB"))
            iteration(groups, groups - 1, groups, last_experts("pe"), alone=True)


def layout(inputs):
    a = {k: np.ascontiguousarray(v) for k, v in inputs.items()}
    tokens = a["x"].shape[0] * S
    c = np.ascontiguousarray

    def rope_columns(w):
        return c(w.reshape(P, 2, NC0, D0 // 2, 2).transpose(0, 2, 1, 4, 3).reshape(P, NC0, P))

    inv_freq = (1.0 / np.float32(10000.0) ** (np.arange(0, D0, 2, dtype=np.float32) / np.float32(D0))).astype(np.float32)
    freqs = (np.arange(S, dtype=np.float32)[None, :] * inv_freq[:, None]).astype(np.float32)
    cos = np.tile(np.cos(freqs), (4, 1)).astype(np.float32)
    sin = np.tile(np.concatenate([np.sin(freqs), -np.sin(freqs)], 0), (2, 1)).astype(np.float32)
    rows = np.arange(P)
    headmask = ((rows % 64) // D1 == np.arange(H // 2)[:, None]).T.astype(np.float32)
    l1 = np.stack([a["L1_xattn_" + n].T for n in ("sa_wq", "sa_wk", "sa_wv", "sa_wo", "ca_wq", "ca_wk", "ca_wv", "ca_wo")], 1)
    w1 = np.concatenate([a["L1_xattn_sh_w1"][None], a["L1_xattn_exp_w1"]], 0)
    w2 = np.concatenate([a["L1_xattn_sh_w2"][None], a["L1_xattn_exp_w2"]], 0)
    return {
        "x": a["x"].reshape(tokens, P), "ctx": a["ctx_1024"].reshape(tokens, P),
        "m0": a["mask_BxS2_bf1"].view(np.uint8), "m1": a["mask_BxSxS_ik0"].reshape(tokens, S),
        "m2": a["mask_BxSxS2_if1"].reshape(tokens, S),
        "wq": rope_columns(a["L0_xattn_Wq"]), "wk": rope_columns(a["L0_xattn_Wk"]), "wv": a["L0_xattn_Wv"],
        "wo": c(a["L0_xattn_Wo"].reshape(NC0, P, P).transpose(1, 0, 2)),
        "gamma": a["L0_xattn_ln_gamma"], "beta": a["L0_xattn_ln_beta"],
        "norms": c(np.stack([a[f"L1_xattn_norm{n}_w"] for n in (1, 2, 3)], 1)),
        "l1w": c(l1), "gw": c(a["L1_xattn_gate_w"].T),
        "w1": c(w1.reshape(NE, HC, P, P).transpose(3, 0, 1, 2).reshape(P, NE * HC, P)),
        "w2": c(w2.reshape(NE, P, HC, P).transpose(3, 0, 2, 1).reshape(P, NE * HC, P)),
        "cos": cos, "sin": sin, "ident": np.eye(P, dtype=np.float32), "headmask": c(headmask),
        "countdown": np.tile(np.arange(E, 0, -1, dtype=np.float32), (P, 1)),
    }


def kernel(**inputs):
    import concourse.bacc as bacc
    from concourse.bass_utils import run_bass_kernel_spmd
    nc = bacc.Bacc("TRN2", target_bir_lowering=False, num_devices=1)
    arrays = {f"in_{k}": v for k, v in layout(inputs).items()}
    aps = [nc.dram_tensor(k, v.shape, mybir.dt.from_np(v.dtype), kind="ExternalInput").ap() for k, v in arrays.items()]
    shape = inputs["x"].shape
    out = nc.dram_tensor("out_y", (shape[0] * shape[1], shape[2]), F32, kind="ExternalOutput").ap()
    build(nc, *aps, out)
    result = run_bass_kernel_spmd(nc, [arrays], core_ids=[0])
    return result.results[0]["out_y"].reshape(shape)
```
